# Optimizing a Trainium2 kernel written in Bass

```python
import numpy as np
import jax
import jax.numpy as jnp

def _softmax(x, axis=-1):
    return jax.nn.softmax(x, axis=axis)

def _gelu(x):
    return jax.nn.gelu(x, approximate=True)

def _silu(x):
    return jax.nn.silu(x)

def _sigmoid(x):
    return jax.nn.sigmoid(x)

def _layernorm(x, axis=-1, eps=1e-05):
    m = jnp.mean(x, axis=axis, keepdims=True)
    v = jnp.var(x, axis=axis, keepdims=True)
    return (x - m) / jnp.sqrt(v + eps)

def _scatter_add(tgt, idx, src, axis=0):
    return tgt.at[idx].add(src)

def _segment_sum(src, seg, n):
    return jax.ops.segment_sum(src, seg, n)
kernel_name = 'mk_decoder_preln_d1_seqx_r8_2cc680'

def setup_inputs(seed: int=0):
    np.random.seed(seed)
    _w = jnp.asarray

    def _rec_inputs():
        import jax
        import jax.numpy as jnp
        _rk = jax.random.key(seed)
        x = -0.0003929 + 0.9999 * jax.random.normal(jax.random.fold_in(_rk, 1), (32, 64, 256), jnp.float32)
        _lenS = 64 - jax.random.randint(jax.random.fold_in(_rk, 7), (32,), 0, max(1, 64 // 4) + 1, jnp.int32)
        _lenS2 = 64 - jax.random.randint(jax.random.fold_in(_rk, 8), (32,), 0, max(1, 64 // 4) + 1, jnp.int32)
        _ctx_2048P = jax.random.normal(jax.random.fold_in(_rk, 11), (32, 16, 256), jnp.float32)
        _ctx_2048c = jax.random.dirichlet(jax.random.fold_in(_rk, 511), 0.3 * jnp.ones((16,), jnp.float32), (32, 64))
        _ctx_2048t = jnp.einsum('bsk,bkd->bsd', _ctx_2048c, _ctx_2048P)
        _ctx_2048t = _ctx_2048t * jax.lax.rsqrt(jnp.mean(jnp.square(_ctx_2048t)) + 1e-12) * 0.953939
        ctx_2048 = -1.39393e-06 + 0.999914 * (_ctx_2048t + 0.3 * jax.random.normal(jax.random.fold_in(_rk, 611), (32, 64, 256), jnp.float32))
        itok_BxS_0_1023 = jax.random.randint(jax.random.fold_in(_rk, 12), (32, 64), 0, 128, jnp.int32)
        return (x, ctx_2048, itok_BxS_0_1023)
    x, ctx_2048, itok_BxS_0_1023 = _rec_inputs()

    def _L0_attn_setup():
        import jax, jax.numpy as jnp
        import numpy as np
        L, N, E, H = (256, 2, 256, 16)
        DH = E // H
        SCALE = DH ** (-0.5)
        key = jax.random.key(seed)
        k1, k2, k3 = jax.random.split(key, 3)
        x = jax.random.normal(k1, (L, N, E), dtype=jnp.float32)
        weight_qkv = jax.random.normal(k2, (3 * E, E), dtype=jnp.float32) * 0.02
        weight_out = jax.random.normal(k3, (E, E), dtype=jnp.float32) * 0.02
        return {'x': x, 'weight_qkv': weight_qkv, 'weight_out': weight_out}
    _L0_attn_all = _L0_attn_setup()
    _L0_attn_in = {k: v for k, v in _L0_attn_all.items() if k in ('weight_qkv', 'weight_out')}
    del _L0_attn_all

    def _L0_xattn_setup():
        import jax, jax.numpy as jnp
        import numpy as np
        B, Lq, Lk = (2, 512, 128)
        Q_DIM, KV_DIM = (256, 256)
        H, HD = (16, 128)
        KVC, QC, R = (64, 96, 64)
        LOOKBACK = 8
        NEG = -1e+30

        def _rope(x, L):
            half = x.shape[-1] // 2
            inv_freq = 1.0 / 10000.0 ** (jnp.arange(half, dtype=jnp.float32) / half)
            ang = jnp.arange(L, dtype=jnp.float32)[:, None] * inv_freq
            cos, sin = (jnp.cos(ang), jnp.sin(ang))
            x1, x2 = (x[..., :half], x[..., half:])
            return jnp.concatenate([x1 * cos - x2 * sin, x1 * sin + x2 * cos], axis=-1)
        key = jax.random.key(seed)
        ks = jax.random.split(key, 11)

        def w(k, shape, fan_in):
            return jax.random.normal(k, shape, jnp.float32) / np.sqrt(fan_in).astype(np.float32)
        return {'q': jax.random.normal(ks[0], (B, Lq, Q_DIM), jnp.float32), 'kv': jax.random.normal(ks[1], (B, Lk, KV_DIM), jnp.float32), 'seg_id': jnp.sort(jax.random.randint(ks[2], (B, Lq), 0, Lk), axis=-1), 'W_kvc': w(ks[3], (KV_DIM, KVC), KV_DIM), 'W_dq': w(ks[4], (Q_DIM, QC), Q_DIM), 'W_uq': w(ks[5], (QC, H * HD), QC), 'W_qr': w(ks[6], (QC, H * R), QC), 'W_uk': w(ks[7], (KVC, H * HD), KVC), 'W_kr': w(ks[8], (KVC, R), KVC), 'W_uv': w(ks[9], (KVC, H * HD), KVC), 'W_o': w(ks[10], (H * HD, Q_DIM), H * HD)}
    _L0_xattn_all = _L0_xattn_setup()
    _L0_xattn_in = {k: v for k, v in _L0_xattn_all.items() if k in ('W_kvc', 'W_dq', 'W_uq', 'W_qr', 'W_uk', 'W_kr', 'W_uv', 'W_o')}
    del _L0_xattn_all

    def _L0_ffn_setup():
        import jax, jax.numpy as jnp
        import numpy as np
        EPS = 1e-08
        QB = 127.0
        key = jax.random.key(seed)
        k1, k2, k3 = jax.random.split(key, 3)
        B, S, DIN, DOUT = (8, 256, 256, 256)
        x = jax.random.normal(k1, (B, S, DIN), dtype=jnp.float32)
        bound = float(np.sqrt(6.0 / DIN))
        weight = jax.random.uniform(k2, (DOUT, DIN), dtype=jnp.float32, minval=-bound, maxval=bound)
        bias = jax.random.normal(k3, (DOUT,), dtype=jnp.float32) * 0.02
        return {'x': x, 'weight': weight, 'bias': bias}
    _L0_ffn_all = _L0_ffn_setup()
    _L0_ffn_in = {k: v for k, v in _L0_ffn_all.items() if k in ('weight', 'bias')}
    del _L0_ffn_all
    return {'x': x, 'ctx_2048': ctx_2048, 'itok_BxS_0_1023': itok_BxS_0_1023, 'L0_attn_weight_qkv': _L0_attn_in['weight_qkv'], 'L0_attn_weight_out': _L0_attn_in['weight_out'], 'L0_xattn_W_kvc': _L0_xattn_in['W_kvc'], 'L0_xattn_W_dq': _L0_xattn_in['W_dq'], 'L0_xattn_W_uq': _L0_xattn_in['W_uq'], 'L0_xattn_W_qr': _L0_xattn_in['W_qr'], 'L0_xattn_W_uk': _L0_xattn_in['W_uk'], 'L0_xattn_W_kr': _L0_xattn_in['W_kr'], 'L0_xattn_W_uv': _L0_xattn_in['W_uv'], 'L0_xattn_W_o': _L0_xattn_in['W_o'], 'L0_ffn_weight': _L0_ffn_in['weight'], 'L0_ffn_bias': _L0_ffn_in['bias']}

def reference(x, ctx_2048, itok_BxS_0_1023, L0_attn_weight_qkv, L0_attn_weight_out, L0_xattn_W_kvc, L0_xattn_W_dq, L0_xattn_W_uq, L0_xattn_W_qr, L0_xattn_W_uk, L0_xattn_W_kr, L0_xattn_W_uv, L0_xattn_W_o, L0_ffn_weight, L0_ffn_bias):
    import jax
    import jax.numpy as jnp

    def _L0_attn_ref(x, weight_qkv, weight_out):
        import jax, jax.numpy as jnp
        import numpy as np
        L, N, E, H = (256, 2, 256, 16)
        DH = E // H
        SCALE = DH ** (-0.5)
        l, n, e = x.shape
        h, dh = (H, DH)
        qkv = jnp.einsum('lne,fe->lnf', x, weight_qkv)
        q, k, v = jnp.split(qkv, 3, axis=-1)
        q = q.reshape(l, n, h, dh) * jnp.asarray(SCALE, x.dtype)
        k = k.reshape(l, n, h, dh)
        v = v.reshape(l, n, h, dh)
        attn = jnp.einsum('lnhd,mnhd->nhlm', q, k)
        causal = jnp.tril(jnp.ones((l, l), dtype=bool))
        attn = jnp.where(causal, attn, jnp.asarray(-jnp.inf, attn.dtype))
        attn = jax.nn.softmax(attn, axis=-1)
        out = jnp.einsum('nhlm,mnhd->lnhd', attn, v).reshape(l, n, e)
        return jnp.einsum('lne,fe->lnf', out, weight_out)

    def _L0_xattn_ref(q, kv, seg_id, W_kvc, W_dq, W_uq, W_qr, W_uk, W_kr, W_uv, W_o):
        import jax, jax.numpy as jnp
        import numpy as np
        B, Lq, Lk = (2, 512, 128)
        Q_DIM, KV_DIM = (256, 256)
        H, HD = (16, 128)
        KVC, QC, R = (64, 96, 64)
        LOOKBACK = 8
        NEG = -1e+30

        def _rope(x, L):
            half = x.shape[-1] // 2
            inv_freq = 1.0 / 10000.0 ** (jnp.arange(half, dtype=jnp.float32) / half)
            ang = jnp.arange(L, dtype=jnp.float32)[:, None] * inv_freq
            cos, sin = (jnp.cos(ang), jnp.sin(ang))
            x1, x2 = (x[..., :half], x[..., half:])
            return jnp.concatenate([x1 * cos - x2 * sin, x1 * sin + x2 * cos], axis=-1)
        b, lq, _ = q.shape
        lk = kv.shape[1]
        kv_c = kv @ W_kvc
        q_c = q @ W_dq
        q_nope = (q_c @ W_uq).reshape(b, lq, H, HD).transpose(0, 2, 1, 3)
        q_rope = (q_c @ W_qr).reshape(b, lq, H, R).transpose(0, 2, 1, 3)
        k_nope = (kv_c @ W_uk).reshape(b, lk, H, HD)
        v = (kv_c @ W_uv).reshape(b, lk, H, HD)
        k_rope = kv_c @ W_kr
        q_rope = _rope(q_rope, lq)
        k_rope = _rope(k_rope, lk)
        scale = 1.0 / np.sqrt(HD + R).astype(np.float32)
        scores = (jnp.einsum('bhqd,bkhd->bhqk', q_nope, k_nope) + jnp.einsum('bhqr,bkr->bhqk', q_rope, k_rope)) * scale
        k_ids = jnp.arange(lk)[None, None, :]
        qs = seg_id[:, :, None]
        good = (k_ids <= qs) & (k_ids >= qs - LOOKBACK)
        scores = jnp.where(good[:, None, :, :], scores, NEG)
        attn = jax.nn.softmax(scores, axis=-1)
        out = jnp.einsum('bhqk,bkhd->bqhd', attn, v).reshape(b, lq, H * HD)
        return out @ W_o

    def _L0_ffn_ref(x, weight, bias):
        import jax, jax.numpy as jnp
        import numpy as np
        EPS = 1e-08
        QB = 127.0
        rms = jnp.sqrt(jnp.mean(x * x, axis=-1, keepdims=True) + EPS)
        xn = x / rms
        gamma = jnp.mean(jnp.abs(weight), axis=-1, keepdims=True)
        w_ternary = jnp.clip(jnp.round(weight / (gamma + EPS)), -1.0, 1.0)
        x_scale = jnp.max(jnp.abs(xn), axis=-1, keepdims=True) / QB
        x_q = jnp.clip(jnp.round(xn / (x_scale + EPS)), -QB, QB)
        out = jnp.einsum('bsk,nk->bsn', x_q, w_ternary)
        out = out * gamma[:, 0] * x_scale
        return out + bias
    x = x + _L0_attn_ref(_layernorm(x, axis=-1), L0_attn_weight_qkv, L0_attn_weight_out)
    x = x + _L0_xattn_ref(_layernorm(x, axis=-1), ctx_2048, itok_BxS_0_1023, L0_xattn_W_kvc, L0_xattn_W_dq, L0_xattn_W_uq, L0_xattn_W_qr, L0_xattn_W_uk, L0_xattn_W_kr, L0_xattn_W_uv, L0_xattn_W_o)
    x = x + _L0_ffn_ref(_layernorm(x, axis=-1), L0_ffn_weight, L0_ffn_bias)
    return x

_drawn_inputs = setup_inputs


def setup_inputs(seed=0):
    import zlib

    import numpy as np

    out = dict(_drawn_inputs(seed))
    spreads = {}
    factors = {'L0_ffn_bias': 4.492}
    for name, (base, spread) in spreads.items():
        noise = np.random.default_rng([zlib.crc32(name.encode()), seed]).standard_normal(out[name].shape)
        drawn = base * np.exp(spread * noise) if base else spread * noise
        out[name] = jnp.asarray(drawn.astype(out[name].dtype))
    for name, factor in factors.items():
        out[name] = (out[name] * factor).astype(out[name].dtype)
    return out
```

```python
from contextlib import ExitStack

import numpy as np

import concourse.bass as bass
from concourse import mybir

P = 128
E = 256
KT = E // P
NT = 16
L, N = 32, 64
H = 16
DH = 16
NPT = P // L
BPT = P // N
HP = H // 2
KVC, QC, R, HD = 64, 96, 64, 128
LOOKBACK = 8
NEG = -1e30
LN_EPS = 1e-5
Q_EPS = 1e-8
QB = 127.0
ROUND = 12582912.0
SELF_SCALE = DH ** -0.5
CROSS_SCALE = float(np.float32(1.0) / np.sqrt(HD + R).astype(np.float32))

ALU = mybir.AluOpType
ACT = mybir.ActivationFunctionType
AX = mybir.AxisListType
F32 = mybir.dt.float32
BF16 = mybir.dt.bfloat16
I32 = mybir.dt.int32


def need(eng, sem, count):
    if not isinstance(count, int) or count > 0:
        eng.wait_ge(sem, count)


def live(t):
    return not isinstance(t, int) or 0 <= t < NT


def upto(t):
    return min(t, NT) if isinstance(t, int) else t


def nth(t, p):
    return 8 * (t - p + 2)


def sweep(eng, step):
    for i in range(-2, 4):
        step(i, i % 2)
    with eng.Fori(2, NT // 2 - 1) as j:
        for p in range(2):
            step(2 * j + p, p)
    for i in range(NT - 2, NT + 4):
        step(i, i % 2)


def decoder_layer(nc, x, ctx_t, seg, w_qkv_t, w_out_t, w_kvc, w_kvc_t, w_dq, w_uq_t, w_qr, w_qr_s,
                  w_uk_t, w_kr, w_kr_s, w_uv_t, w_o, w_ff, b_ff, ident_c, causal_c, parity_c,
                  cos_c, sin_c, kidx_c, x1_dram, out):
    with ExitStack() as ctx:
        def sb(name, shape, dt=F32):
            return ctx.enter_context(nc.sbuf_tensor(name, shape, dt))

        def sem(name):
            return ctx.enter_context(nc.semaphore(name))

        bank = [ctx.enter_context(nc.psum_tensor(f"bank{i}", [P, 512], F32)) for i in range(4)]
        quad = ctx.enter_context(nc.psum_tensor("quad", [P, 4, 512], F32))

        ident = sb("ident", [P, P])
        ident_b = sb("ident_b", [P, P], BF16)
        ones = sb("ones", [P, P])
        neg_half = sb("neg_half", [P, 1])
        ln_eps = sb("ln_eps", [P, 1])
        causal = sb("causal", [P, L])
        parity = sb("parity", [P, 2])
        cos_t = sb("cos_t", [P, N])
        sin_t = sb("sin_t", [P, N])
        kidx = sb("kidx", [P, N])
        seg_i = sb("seg_i", [P, NT], I32)
        seg_f = sb("seg_f", [P, NT])
        window = sb("window", [P, NT, N])
        window2 = sb("window2", [P, NT, N])
        wqkv = sb("wqkv", [P, KT, 3 * E])
        wout_n = sb("wout_n", [P, KT, E])
        wout = sb("wout", [P, KT, 2, E])
        wkvc2 = sb("wkvc2", [P, KT, 2, KVC])
        wkvc_t = sb("wkvc_t", [KVC, E])
        wdq = sb("wdq", [P, KT, QC])
        wuq_t = sb("wuq_t", [P, H, QC])
        wuk_t = sb("wuk_t", [P, H, KVC])
        wqr = sb("wqr", [QC, H * R])
        wqr_s = sb("wqr_s", [QC, H * R])
        wkr = sb("wkr", [KVC, R])
        wkr_s = sb("wkr_s", [KVC, R])
        wkr2 = sb("wkr2", [P, KT, 2, R])
        wkr2_s = sb("wkr2_s", [P, KT, 2, R])
        wuv_t = sb("wuv_t", [P, H, KVC])
        qn_qr = sb("qn_qr", [P, 2, 2, HP, P])
        qn, qr = qn_qr[:, 0, :, :, :], qn_qr[:, 1, :, :, :]
        wo = qn_qr[:, :, :, :, :].rearrange("p a b h t -> p (a b h t)").rearrange("p (h e) -> p h e", h=H)
        wqn = sb("wqn", [QC, HP, 2 * KVC])
        wvo = sb("wvo", [P, HP, E])
        wff = sb("wff", [P, KT, E])
        wff_n = sb("wff_n", [P, KT, E])
        wff_q = sb("wff_q", [P, KT, E], BF16)
        wff_t = sb("wff_t", [P, KT, E], BF16)
        gamma = sb("gamma", [P, KT])
        gamma_e = sb("gamma_e", [P, KT])
        gamma_r = sb("gamma_r", [P, KT])
        gamma_d = sb("gamma_d", [P, KT, P])
        gamma_b = sb("gamma_b", [P, E])
        bias_b = sb("bias_b", [P, E])

        xall = sb("xall", [P, NT, E])
        stat = sb("stat", [P, 2, 6])
        mv = sb("mv", [P, 2, 2])
        ve = sb("ve", [P, 2, 1])
        rstd = sb("rstd", [P, 2, 1])
        xh = sb("xh", [P, 2, E])
        xt = sb("xt", [P, 2, KT, P])
        qt = sb("qt", [P, 2, 2, P])
        kx = sb("kx", [P, 2, 2, 2, P])
        vs = sb("vs", [P, 2, E])
        sm = sb("sm", [P, 2, 1024])
        sd = sb("sd", [P, 2, 1024])
        pe = sb("pe", [P, 2, 1024])
        pn = sb("pn", [P, 2, 1024])
        mx = sb("mx", [P, 2, H])
        rs = sb("rs", [P, 2, H])
        ri = sb("ri", [P, 2, H])
        pt = sb("pt", [P, 2, 1024])
        ot = sb("ot", [P, 2, 4, P])
        x1 = sb("x1", [P, 2, E])
        ctxt = sb("ctxt", [P, 2, KT, P])
        kn = sb("kn", [P, 2, P])
        kr = sb("kr", [P, 2, P])
        kr_a = sb("kr_a", [P, P])
        kr_b = sb("kr_b", [P, P])
        kvn = sb("kvn", [P, 2, 2, P])
        qct = sb("qct", [QC, 2, P])
        qr_a = sb("qr_a", [P, 2, 512])
        qr_b = sb("qr_b", [P, 2, 512])
        ctxo = sb("ctxo", [P, 2, HP, P])
        x2 = sb("x2", [P, 2, E])
        x2b = sb("x2b", [P, 2, E])
        stat3 = sb("stat3", [P, 2, 6])
        mv3 = sb("mv3", [P, 2, 2])
        ve3 = sb("ve3", [P, 2, 1])
        rstd3 = sb("rstd3", [P, 2, 1])
        h3 = sb("h3", [P, 2, E])
        hsq = sb("hsq", [P, 2, E])
        ssq = sb("ssq", [P, 2, 1])
        mh = sb("mh", [P, 2, 1])
        vq = sb("vq", [P, 2, 1])
        rq = sb("rq", [P, 2, 1])
        xs = sb("xs", [P, 2, 1])
        xse = sb("xse", [P, 2, 1])
        xsr = sb("xsr", [P, 2, 1])
        fq = sb("fq", [P, 2, 1])
        hr = sb("hr", [P, 2, E])
        hc = sb("hc", [P, 2, E])
        xq = sb("xq", [P, 2, E], BF16)
        xqt = sb("xqt", [P, 2, KT, P], BF16)
        ffs = sb("ffs", [P, 2, E])
        res = sb("res", [P, 2, E])

        in_consts, in_attn_w, in_cross_w, in_ffn_w, in_seg = (sem(s) for s in (
            "in_consts", "in_attn_w", "in_cross_w", "in_ffn_w", "in_seg"))
        fills = sem("fills")
        pe_begun, dve_begun = sem("pe_begun"), sem("dve_begun")
        ident_b_made, seg_made, wout_made, window_steps, ternary_steps, products_ps, products = (sem(s) for s in (
            "ident_b_made", "seg_made", "wout_made", "window_steps", "ternary_steps", "products_ps", "products"))
        x_in = [sem(f"x_in{p}") for p in range(2)]
        x1_out = [sem(f"x1_out{p}") for p in range(2)]
        x1_in = [sem(f"x1_in{p}") for p in range(2)]
        ctx_in = [sem(f"ctx_in{p}") for p in range(2)]
        out_done = [sem(f"out_done{p}") for p in range(2)]
        a_stat, a_mean, a_var, a_rstd, a_xh = (sem(s) for s in ("a_stat", "a_mean", "a_var", "a_rstd", "a_xh"))
        a_xt_ps, a_xt, a_qk_ps, a_qk, a_v_ps, a_v = (sem(s) for s in (
            "a_xt_ps", "a_xt", "a_qk_ps", "a_qk", "a_v_ps", "a_v"))
        a_s_ps, a_masked, a_max, a_diff, a_exp, a_sum, a_rec, a_norm, a_pt = (sem(s) for s in (
            "a_s_ps", "a_masked", "a_max", "a_diff", "a_exp", "a_sum", "a_rec", "a_norm", "a_pt"))
        a_o_ps, a_o, a_y_ps, a_x1 = (sem(s) for s in ("a_o_ps", "a_o", "a_y_ps", "a_x1"))
        b_stat, b_mean, b_var, b_rstd, b_xh = (sem(s) for s in ("b_stat", "b_mean", "b_var", "b_rstd", "b_xh"))
        b_xt_ps, b_xt, b_qc_ps, b_qc = (sem(s) for s in ("b_xt_ps", "b_xt", "b_qc_ps", "b_qc"))
        b_kn, b_kr_ab, b_kr, b_kvn_ps, b_kvn = (sem(s) for s in (
            "b_kn", "b_kr_ab", "b_kr", "b_kvn_ps", "b_kvn"))
        b_proj_ps, b_qn, b_rope, b_qr = (sem(s) for s in ("b_proj_ps", "b_qn", "b_rope", "b_qr"))
        b_s_ps, b_masked, b_max, b_diff, b_exp, b_sum, b_rec, b_norm = (sem(s) for s in (
            "b_s_ps", "b_masked", "b_max", "b_diff", "b_exp", "b_sum", "b_rec", "b_norm"))
        b_pt_ps, b_pt, b_c_ps, b_c, b_y_ps = (sem(s) for s in ("b_pt_ps", "b_pt", "b_c_ps", "b_c", "b_y_ps"))
        c_x2, c_x2b, c_stat, c_mean, c_var, c_rstd, c_h, c_ssq, c_mh = (sem(s) for s in (
            "c_x2", "c_x2b", "c_stat", "c_mean", "c_var", "c_rstd", "c_h", "c_ssq", "c_mh"))
        c_vq, c_rq, c_scale, c_xq = (sem(s) for s in ("c_vq", "c_rq", "c_scale", "c_xq"))
        c_t_ps, c_t, c_y_ps, c_ffs, c_out = (sem(s) for s in ("c_t_ps", "c_t", "c_y_ps", "c_ffs", "c_out"))

        x_cols = x.rearrange("l (t n) e -> t n l e", n=NPT)
        x1_cols = x1_dram.rearrange("l (t n) e -> t n l e", n=NPT)
        x1_rows = x1_dram.rearrange("(t b) n e -> t (b n) e", b=BPT)
        out_rows = out.rearrange("(t b) n e -> t (b n) e", b=BPT)

        a_t = bank[0][:, 0:E].rearrange("p (k t) -> p k t", k=KT)
        a_qkp = bank[1][:, :].rearrange("p (f t) -> p f t", f=4)
        a_vp = bank[2][:, 0:E]
        a_y = bank[3][:, 0:E]
        b_t = bank[2][:, 0:E].rearrange("p (k t) -> p k t", k=KT)
        b_qcp = bank[2][0:QC, E:E + P]
        b_y = bank[2][:, 0:E]
        b_knp = bank[3][:, 0:P]
        b_krp = bank[3][:, P:3 * P].rearrange("p (s t) -> p s t", s=2)
        b_kvnp = bank[3][:, 3 * P:3 * P + KVC]
        c_tp = bank[3][:, 0:P].bitcast(BF16).rearrange("p (k t) -> p k t", k=KT)
        c_yp = bank[3][:, 0:E]

        block = ctx.enter_context(nc.Block())

        @block.sync
        def _(eng):
            for dst, src in ((ident, ident_c), (causal, causal_c), (parity, parity_c), (cos_t, cos_c),
                             (sin_t, sin_c), (kidx, kidx_c)):
                eng.dma_start(dst[:, :], src).then_inc(in_consts, 16)

            def load_x(t, p):
                need(eng, a_stat, t - 1)
                eng.dma_start(xall[:, t, :], x_cols[t]).then_inc(x_in[p], 16)

            load_x(0, 0)
            load_x(1, 1)
            eng.dma_start(wqkv[:, :, :], w_qkv_t.rearrange("(k p) f -> p k f", p=P)).then_inc(in_attn_w, 16)
            eng.dma_start(wout_n[:, :, :], w_out_t.rearrange("(k p) f -> p k f", p=P)).then_inc(in_attn_w, 16)
            eng.dma_start(seg_i[:, :], seg).then_inc(in_seg, 16)
            eng.dma_start(wff[:, :, :], w_ff.rearrange("(k p) f -> p k f", p=P)).then_inc(in_ffn_w, 16)
            eng.dma_start(bias_b[:, :], b_ff.to_broadcast([P, E])).then_inc(in_ffn_w, 16)
            for d in range(2):
                eng.dma_start(wkvc2[:, :, d, :], w_kvc.rearrange("(k p) c -> p k c", p=P)).then_inc(in_cross_w, 16)
            for dst, src in ((wkvc_t, w_kvc_t), (wqr, w_qr), (wqr_s, w_qr_s), (wkr, w_kr), (wkr_s, w_kr_s)):
                eng.dma_start(dst[:, :], src).then_inc(in_cross_w, 16)
            eng.dma_start(wdq[:, :, :], w_dq.rearrange("(k p) c -> p k c", p=P)).then_inc(in_cross_w, 16)
            for dst, src in ((wuq_t[:, :, :], w_uq_t), (wuk_t[:, :, :], w_uk_t), (wuv_t[:, :, :], w_uv_t), (wo, w_o)):
                eng.dma_start(dst, src).then_inc(in_cross_w, 16)

            def store_x1(t, p):
                eng.wait_ge(a_x1, t + 1)
                eng.dma_start(x1_cols[t], x1[:, p, :]).then_inc(x1_out[p], 16)

            def step_a(i, p):
                if live(i + 2) and not (isinstance(i, int) and i < 0):
                    load_x(i + 2, p)
                if live(i - 1):
                    store_x1(i - 1, 1 - p)

            sweep(eng, step_a)

            for p in range(2):
                eng.wait_ge(x1_out[p], 16 * NT // 2)

            def load_b(t, p):
                need(eng, b_stat, t - 1)
                eng.dma_start(xall[:, t, :], x1_rows[t]).then_inc(x1_in[p], 16)
                need(eng, b_kvn_ps, t - 1)
                eng.dma_start(ctxt[:, p, :, :], ctx_t[t].rearrange("p (k t) -> p k t", k=KT)).then_inc(ctx_in[p], 16)

            def store_out(t, p):
                eng.wait_ge(c_out, t + 1)
                eng.dma_start(out_rows[t], res[:, p, :]).then_inc(out_done[p], 16)

            def step_b(i, p):
                if live(i + 2):
                    load_b(i + 2, p)
                if live(i - 3):
                    store_out(i - 3, 1 - p)

            sweep(eng, step_b)
            for p in range(2):
                eng.wait_ge(out_done[p], 16 * NT // 2)

        @block.gpsimd
        def _(eng):
            eng.memset(ones[:, :], 1.0).then_inc(fills, 1)
            eng.memset(neg_half[:, :], -0.5).then_inc(fills, 1)
            eng.memset(kvn[:, :, :, :], 0.0).then_inc(fills, 1)
            eng.memset(ln_eps[:, :], LN_EPS).then_inc(fills, 1)
            eng.wait_ge(fills, 4)
            eng.wait_ge(seg_made, 1)
            eng.wait_ge(in_consts, 96)
            eng.tensor_tensor(window[:, :, :], kidx[:, None, :].to_broadcast([P, NT, N]),
                              seg_f[:, :, None].to_broadcast([P, NT, N]), ALU.subtract).then_inc(window_steps, 1)
            eng.wait_ge(window_steps, 1)
            eng.tensor_scalar(window2[:, :, :], window[:, :, :], 0.0, NEG, ALU.is_gt, ALU.mult).then_inc(window_steps, 1)
            eng.wait_ge(window_steps, 2)
            eng.tensor_scalar(window[:, :, :], window[:, :, :], -float(LOOKBACK), NEG, ALU.is_lt, ALU.mult).then_inc(window_steps, 1)
            eng.wait_ge(window_steps, 3)
            eng.tensor_tensor(window[:, :, :], window[:, :, :], window2[:, :, :], ALU.add).then_inc(window_steps, 1)

            def inverse_root(t, p, mean, mvt, vet, var, rt, done):
                eng.wait_ge(mean, t + 1)
                eng.tensor_tensor(vet[:, p, :], mvt[:, p, 1:2], ln_eps[:, :], ALU.add).then_inc(var, 1)
                eng.wait_ge(var, t + 1)
                eng.tensor_tensor(rt[:, p, :], vet[:, p, :], neg_half[:, :], ALU.pow).then_inc(done, 1)

            def submax(t, p, width, maxed, exped, done):
                eng.wait_ge(maxed, t + 1)
                need(eng, exped, t - 1)
                m = H * width
                eng.tensor_tensor(sd[:, p, 0:m].rearrange("p (h k) -> p h k", h=H),
                                  sm[:, p, 0:m].rearrange("p (h k) -> p h k", h=H),
                                  mx[:, p, :, None].to_broadcast([P, H, width]), ALU.subtract).then_inc(done, 1)

            def normalise(t, p, width, recip, used, uses, done):
                eng.wait_ge(recip, t + 1)
                need(eng, used, uses * (t - 1))
                m = H * width
                eng.tensor_tensor(pn[:, p, 0:m].rearrange("p (h k) -> p h k", h=H),
                                  pe[:, p, 0:m].rearrange("p (h k) -> p h k", h=H),
                                  ri[:, p, :, None].to_broadcast([P, H, width]), ALU.mult).then_inc(done, 1)

            def step_a(i, p):
                if live(i):
                    submax(i, p, L, a_max, a_exp, a_diff)
                if live(i + 2):
                    inverse_root(i + 2, p, a_mean, mv, ve, a_var, rstd, a_rstd)
                if live(i):
                    normalise(i, p, L, a_rec, a_pt, 1, a_norm)

            sweep(eng, step_a)

            def add_rope(t, p, s):
                eng.wait_ge(b_rope, 4 * t + 2 * s + 2)
                need(eng, b_s_ps, t - 1)
                eng.tensor_tensor(qr[:, p, 4 * s:4 * s + 4, :].rearrange("p h t -> p (h t)"), qr_a[:, s, :], qr_b[:, s, :], ALU.add).then_inc(b_qr, 1)

            def biased(t, p):
                eng.wait_ge(c_x2, t + 1)
                need(eng, c_out, t - 1)
                eng.tensor_tensor(x2b[:, p, :], x2[:, p, :], bias_b[:, :], ALU.add).then_inc(c_x2b, 1)

            def inverse_rms(t, p):
                need(eng, c_xq, t - 1)
                eng.wait_ge(c_vq, t + 1)
                eng.tensor_tensor(rq[:, p, :], vq[:, p, :], neg_half[:, :], ALU.pow).then_inc(c_rq, 1)

            def step_b(i, p):
                if live(i - 2):
                    inverse_root(i - 2, p, c_mean, mv3, ve3, c_var, rstd3, c_rstd)
                    biased(i - 2, p)
                    inverse_rms(i - 2, p)
                if live(i):
                    submax(i, p, N, b_max, b_exp, b_diff)
                if live(i + 2):
                    inverse_root(i + 2, p, b_mean, mv, ve, b_var, rstd, b_rstd)
                if live(i + 1):
                    add_rope(i + 1, 1 - p, 0)
                    add_rope(i + 1, 1 - p, 1)
                if live(i):
                    normalise(i, p, N, b_rec, b_pt_ps, 2, b_norm)

            eng.wait_ge(in_ffn_w, 32)
            sweep(eng, step_b)

        @block.scalar
        def _(eng):
            eng.wait_ge(in_consts, 96)
            eng.activation(ident_b[:, :], ident[:, :], ACT.Copy).then_inc(ident_b_made, 1)

            def x_t(t, p, made, used, done, src):
                eng.wait_ge(made, t + 1)
                need(eng, used, t - 1)
                eng.activation(xt[:, p, :, :], src, ACT.Copy).then_inc(done, 1)

            def heads_out(t, p):
                eng.wait_ge(a_o_ps, t + 1)
                need(eng, a_y_ps, t - 1)
                eng.activation(ot[:, p, :, :].rearrange("p g (n l) -> p n g l", n=NPT),
                               quad[:, :, 0:P].rearrange("p n (g l) -> p n g l", g=4), ACT.Copy).then_inc(a_o, 1)

            def exps(t, p, width, scale, diff, normed, done):
                eng.wait_ge(diff, t + 1)
                need(eng, normed, t - 1)
                eng.activation(pe[:, p, 0:H * width], sd[:, p, 0:H * width], ACT.Exp, scale=scale).then_inc(done, 1)

            def queries_keys(t, p):
                eng.wait_ge(a_qk_ps, t + 1)
                need(eng, a_s_ps, t - 1)
                eng.activation(qt[:, p, :, :], a_qkp[:, 0:2, :], ACT.Copy)
                for j in range(2):
                    last = eng.activation(kx[:, p, :, j, :], a_qkp[:, 2:4, :], ACT.Copy, scale=parity[:, j:j + 1])
                last.then_inc(a_qk, 1)

            def values(t, p):
                eng.wait_ge(a_v_ps, t + 1)
                need(eng, a_o_ps, t - 1)
                eng.activation(vs[:, p, :], a_vp, ACT.Copy).then_inc(a_v, 1)

            def step_a(i, p):
                if live(i + 1):
                    x_t(i + 1, 1 - p, a_xt_ps, a_v_ps, a_xt, a_t)
                if live(i - 1):
                    heads_out(i - 1, 1 - p)
                if live(i + 1):
                    queries_keys(i + 1, 1 - p)
                if live(i):
                    exps(i, p, L, SELF_SCALE, a_diff, a_norm, a_exp)
                if live(i + 1):
                    values(i + 1, 1 - p)

            sweep(eng, step_a)

            for g in range(4):
                eng.wait_ge(products_ps, 2 * g + 1)
                eng.activation(wqn[:, 2 * g:2 * g + 2, :].rearrange("q h c -> q (h c)"), bank[0][0:QC, 0:4 * KVC], ACT.Copy).then_inc(products, 1)
                eng.wait_ge(products_ps, 2 * g + 2)
                eng.activation(wvo[:, 2 * g:2 * g + 2, :].rearrange("q h c -> q (h c)"), bank[1][:, :], ACT.Copy).then_inc(products, 1)
            eng.wait_ge(products_ps, 9)
            for k in range(KT):
                for d in range(2):
                    eng.activation(wkr2[:, k, d, :], bank[2][:, k * R:(k + 1) * R], ACT.Copy)
                    last = eng.activation(wkr2_s[:, k, d, :], bank[2][:, (2 + k) * R:(3 + k) * R], ACT.Copy)
            last.then_inc(products, 1)
            eng.wait_ge(products_ps, 10)
            eng.activation(wff_t[:, :, :], quad[:, 0, 0:E].bitcast(BF16).rearrange("p (k n) -> p k n", k=KT), ACT.Copy).then_inc(products, 1)
            eng.wait_ge(products_ps, 11)
            eng.activation(gamma_b[:, :], quad[:, 1, 0:E], ACT.Copy).then_inc(products, 1)

            def keys_nope(t, p):
                eng.wait_ge(b_kvn_ps, t + 1)
                need(eng, b_s_ps, t - 1)
                eng.activation(kn[:, p, :], b_knp, ACT.Copy).then_inc(b_kn, 1)

            def keys_rows(t, p):
                eng.wait_ge(b_kvn_ps, t + 1)
                need(eng, b_c_ps, 2 * (t - 1))
                for b in range(BPT):
                    for d in range(2):
                        last = eng.activation(kvn[64 * d:64 * d + 64, p, b, 64 * d:64 * d + 64],
                                              b_kvnp[64 * b:64 * b + 64, :], ACT.Copy)
                last.then_inc(b_kvn, 1)

            def p_t(t, p, s):
                eng.wait_ge(b_pt_ps, 2 * t + s + 1)
                need(eng, b_c_ps, 2 * (t - 1))
                eng.activation(pt[:, p, 512 * s:512 * s + 512], quad[:, 2 + s, :], ACT.Copy).then_inc(b_pt, 1)

            def q_c(t, p):
                eng.wait_ge(b_qc_ps, t + 1)
                need(eng, b_proj_ps, 6 * (t - 1))
                eng.activation(qct[:, p, :], b_qcp, ACT.Copy).then_inc(b_qc, 1)

            def contexts(t, p, b):
                eng.wait_ge(b_c_ps, 2 * t + b + 1)
                need(eng, b_y_ps, t - 1)
                eng.activation(ctxo[:, p, :, 64 * b:64 * b + 64], quad[:, 2 + b, :].rearrange("p (h q) -> p h q", h=HP),
                               ACT.Copy).then_inc(b_c, 1)

            def queries_nope(t, p, s):
                eng.wait_ge(b_proj_ps, 6 * t + s + 1)
                need(eng, b_s_ps, t - 1)
                eng.activation(qn[:, p, 4 * s:4 * s + 4, :].rearrange("p h t -> p (h t)"), bank[s][:, :],
                               ACT.Copy).then_inc(b_qn, 1)

            def squares(t, p):
                eng.wait_ge(c_h, t + 1)
                need(eng, c_vq, t - 1)
                eng.activation(hsq[:, p, :], h3[:, p, :], ACT.Square, accum_out=ssq[:, p, :]).then_inc(c_ssq, 1)
                eng.wait_ge(c_ssq, t + 1)
                need(eng, c_rq, t - 1)
                eng.activation(vq[:, p, :], ssq[:, p, :], ACT.Copy, scale=1.0 / E, bias=Q_EPS).then_inc(c_vq, 1)

            def x_q_t(t, p):
                eng.wait_ge(c_t_ps, t + 1)
                need(eng, c_y_ps, t - 1)
                eng.activation(xqt[:, p, :, :], c_tp, ACT.Copy).then_inc(c_t, 1)

            def step_b(i, p):
                if live(i - 2):
                    squares(i - 2, p)
                if live(i + 1):
                    x_t(i + 1, 1 - p, b_xt_ps, b_qc_ps, b_xt, b_t)
                    keys_nope(i + 1, 1 - p)
                if live(i - 1):
                    p_t(i - 1, 1 - p, 0)
                    p_t(i - 1, 1 - p, 1)
                if live(i + 1):
                    q_c(i + 1, 1 - p)
                if live(i - 1):
                    contexts(i - 1, 1 - p, 0)
                    contexts(i - 1, 1 - p, 1)
                if live(i + 1):
                    keys_rows(i + 1, 1 - p)
                    queries_nope(i + 1, 1 - p, 0)
                    queries_nope(i + 1, 1 - p, 1)
                if live(i):
                    exps(i, p, N, CROSS_SCALE, b_diff, b_norm, b_exp)
                if live(i - 2):
                    x_q_t(i - 2, p)

            sweep(eng, step_b)

        @block.tensor
        def _(eng):
            def transpose_x(t, p, ready, freed, free_at, dst, done):
                eng.wait_ge(ready, t + 1)
                need(eng, freed, free_at)
                for k in range(KT):
                    last = eng.transpose(dst[:, k, :], xh[:, p, k * P:(k + 1) * P], ident[:, :])
                last.then_inc(done, 1)

            def qkv(t, p):
                eng.wait_ge(a_xt, t + 1)
                need(eng, a_qk, t)
                for f in range(4):
                    for k in range(KT):
                        last = eng.matmul(a_qkp[:, f, :], wqkv[:, k, f * P:(f + 1) * P], xt[:, p, k, :],
                                          start=k == 0, stop=k == KT - 1)
                last.then_inc(a_qk_ps, 1)
                need(eng, a_v, t)
                for k in range(KT):
                    last = eng.matmul(a_vp, xt[:, p, k, :], wqkv[:, k, 2 * E:3 * E], start=k == 0, stop=k == KT - 1)
                last.then_inc(a_v_ps, 1)

            def scores_a(t, p):
                eng.wait_ge(a_qk, t + 1)
                need(eng, a_masked, t)
                need(eng, a_o, t - 1)
                eng.sem_inc(pe_begun, 1)
                for g in range(2):
                    for n in range(NPT):
                        for r in range(4):
                            last = eng.matmul(quad[32 * n:32 * n + 32, r, g * 64:g * 64 + 64],
                                              qt[32 * r:32 * r + 32, p, g, 32 * n:32 * n + 32],
                                              kx[32 * r:32 * r + 32, p, g, :, 32 * n:32 * n + 32],
                                              start=True, stop=True)
                last.then_inc(a_s_ps, 1)

            def weigh_a(t, p):
                eng.wait_ge(a_masked, upto(t + 2))
                eng.wait_ge(a_v, t + 1)
                eng.wait_ge(a_pt, t + 1)
                eng.sem_inc(pe_begun, 1)
                ptv = pt[:, p, 0:512].rearrange("p (r g c) -> p r g c", r=4, g=2)
                for g in range(2):
                    for r in range(4):
                        for n in range(NPT):
                            last = eng.matmul(quad[32 * r:32 * r + 32, n, g * 64:g * 64 + 64],
                                              vs[32 * n:32 * n + 32, p, 32 * (4 * g + r):32 * (4 * g + r) + 32],
                                              ptv[32 * n:32 * n + 32, r, g, :], start=True, stop=True)
                last.then_inc(a_o_ps, 1)

            def project_a(t, p):
                eng.wait_ge(a_o, t + 1)
                need(eng, a_x1, t)
                for g in range(2):
                    for j in range(2):
                        last = eng.matmul(a_y, ot[:, p, 2 * g + j, :], wout[:, g, j, :],
                                          start=g + j == 0, stop=g + j == 2)
                last.then_inc(a_y_ps, 1)

            def step_a(i, p):
                if live(i):
                    scores_a(i, p)
                if live(i + 1):
                    transpose_x(i + 1, 1 - p, a_xh, a_xt, i + 1, a_t, a_xt_ps)
                if live(i - 1):
                    weigh_a(i - 1, 1 - p)
                if live(i + 1):
                    qkv(i + 1, 1 - p)
                if live(i - 1):
                    project_a(i - 1, 1 - p)

            eng.wait_ge(in_consts, 96)
            eng.wait_ge(in_attn_w, 32)
            eng.wait_ge(wout_made, 2)
            sweep(eng, step_a)

            eng.wait_ge(in_cross_w, 16 * 12)
            for g in range(4):
                need(eng, products, 2 * g - 1)
                for h in range(4):
                    last = eng.matmul(bank[0][0:QC, h * KVC:(h + 1) * KVC], wuq_t[:, 4 * g + h, :], wuk_t[:, 4 * g + h, :],
                                      start=True, stop=True)
                last.then_inc(products_ps, 1)
                need(eng, products, 2 * g)
                for h in range(4):
                    c = 64 * (h % 2)
                    last = eng.matmul(bank[1][c:c + KVC, (h // 2) * E:(h // 2 + 1) * E], wuv_t[:, 4 * g + h, :], wo[:, 4 * g + h, :],
                                      start=True, stop=True)
                last.then_inc(products_ps, 1)
            for s, w in enumerate((wkr, wkr_s)):
                for k in range(KT):
                    last = eng.matmul(bank[2][:, (2 * s + k) * R:(2 * s + k + 1) * R], wkvc_t[:, k * P:(k + 1) * P], w[:, :],
                                      start=True, stop=True)
            last.then_inc(products_ps, 1)
            eng.wait_ge(ident_b_made, 1)
            eng.wait_ge(ternary_steps, 6)
            tern = quad[:, 0, 0:E].bitcast(BF16).rearrange("p (k n) -> p k n", k=KT)
            for k in range(KT):
                for n in range(KT):
                    last = eng.transpose(tern[:, k, n * P:(n + 1) * P], wff_q[:, n, k * P:(k + 1) * P], ident_b[:, :])
            last.then_inc(products_ps, 1)
            for n in range(KT):
                last = eng.matmul(quad[:, 1, n * P:(n + 1) * P], ones[:, :], gamma_d[:, n, :], start=True, stop=True)
            last.then_inc(products_ps, 1)

            def keys(t, p):
                eng.wait_ge(ctx_in[p], nth(t, p))
                need(eng, c_ffs, t - 3)
                for dst, w in ((b_knp, wkvc2), (b_krp[:, 0, :], wkr2), (b_krp[:, 1, :], wkr2_s)):
                    for k in range(KT):
                        last = eng.matmul(dst, w[:, k, :, :].rearrange("p d c -> p (d c)"), ctxt[:, p, k, :],
                                          start=k == 0, stop=k == KT - 1)
                for k in range(KT):
                    last = eng.matmul(b_kvnp, ctxt[:, p, k, :], wkvc2[:, k, 0, :], start=k == 0, stop=k == KT - 1)
                last.then_inc(b_kvn_ps, 1)

            def q_c(t, p):
                eng.wait_ge(b_xt, t + 1)
                for k in range(KT):
                    last = eng.matmul(b_qcp, wdq[:, k, :], xt[:, p, k, :], start=k == 0, stop=k == KT - 1)
                last.then_inc(b_qc_ps, 1)

            def queries(t, p):
                eng.wait_ge(b_qc, t + 1)
                frees = ((b_rope, 4 * t - 1), (b_rope, 4 * t), (b_qn, 2 * t + 1), (b_qn, 2 * t + 2),
                         (b_rope, 4 * t + 1), (b_rope, 4 * t + 2))
                wn = wqn[:, :, :].rearrange("q h c -> q (h c)")
                for s, (w, first) in enumerate(((wn, 0), (wn, 4), (wqr, 0), (wqr_s, 0), (wqr, 4), (wqr_s, 4))):
                    need(eng, *frees[s])
                    for h in range(4):
                        c = (first + h) * P
                        last = eng.matmul(bank[s % 2][:, h * P:(h + 1) * P], w[:, c:c + P], qct[:, p, :],
                                          start=True, stop=True)
                    last.then_inc(b_proj_ps, 1)

            def scores_b(t, p):
                eng.wait_ge(b_qn, 2 * t + 2)
                eng.wait_ge(b_qr, 2 * t + 2)
                eng.wait_ge(b_kn, t + 1)
                eng.wait_ge(b_kr, t + 1)
                need(eng, b_masked, t)
                eng.sem_inc(pe_begun, 1)
                for h in range(HP):
                    for part, (q, k) in enumerate(((qn, kn), (qr, kr))):
                        for b in range(BPT):
                            for s in range(2):
                                rows = slice(64 * s, 64 * s + 64)
                                last = eng.matmul(quad[64 * b:64 * b + 64, s, h * N:(h + 1) * N],
                                                  q[rows, p, h, 64 * b:64 * b + 64], k[rows, p, 64 * b:64 * b + 64],
                                                  start=part == 0, stop=part == 1)
                last.then_inc(b_s_ps, 1)

            def turn_p(t, p, s):
                eng.wait_ge(b_norm, t + 1)
                need(eng, b_c, 2 * t)
                for h in range(4):
                    last = eng.transpose(quad[:, 2 + s, h * P:(h + 1) * P], pn[:, p, (4 * s + h) * P:(4 * s + h + 1) * P],
                                         ident[:, :])
                last.then_inc(b_pt_ps, 1)

            def weigh_b(t, p):
                eng.wait_ge(b_kvn, t + 1)
                eng.wait_ge(b_pt, 2 * t + 2)
                pv = pt[:, p, :].rearrange("p (h b q) -> p h b q", h=HP, b=BPT)
                for b in range(BPT):
                    eng.matmul(quad[:, 2 + b, :].rearrange("p (h q) -> p h q", h=HP), kvn[:, p, b, :], pv[:, :, b, :],
                               start=True, stop=True).then_inc(b_c_ps, 1)

            def project_b(t, p):
                eng.wait_ge(b_c, 2 * t + 2)
                eng.wait_ge(b_qc, upto(t + 3))
                for h in range(HP):
                    last = eng.matmul(b_y, ctxo[:, p, h, :], wvo[:, h, :], start=h == 0, stop=h == HP - 1)
                last.then_inc(b_y_ps, 1)

            def feed_forward(t, p):
                eng.wait_ge(b_kr, upto(t + 4))
                eng.wait_ge(b_kvn, upto(t + 4))
                eng.wait_ge(c_xq, t + 1)
                for k in range(KT):
                    last = eng.transpose(c_tp[:, k, :], xq[:, p, k * P:(k + 1) * P], ident_b[:, :])
                last.then_inc(c_t_ps, 1)
                eng.wait_ge(c_t, t + 1)
                for k in range(KT):
                    last = eng.matmul(c_yp, xqt[:, p, k, :], wff_t[:, k, :], start=k == 0, stop=k == KT - 1)
                last.then_inc(c_y_ps, 1)

            def step_b(i, p):
                if live(i):
                    scores_b(i, p)
                if live(i + 1):
                    transpose_x(i + 1, 1 - p, b_xh, c_x2, i - 1, b_t, b_xt_ps)
                    keys(i + 1, 1 - p)
                if live(i - 1):
                    turn_p(i - 1, 1 - p, 0)
                    turn_p(i - 1, 1 - p, 1)
                if live(i + 1):
                    q_c(i + 1, 1 - p)
                if live(i - 1):
                    weigh_b(i - 1, 1 - p)
                if live(i + 1):
                    queries(i + 1, 1 - p)
                if live(i - 1):
                    project_b(i - 1, 1 - p)
                if live(i - 2):
                    feed_forward(i - 2, p)

            eng.wait_ge(products, 11)
            sweep(eng, step_b)

        @block.vector
        def _(eng):
            eng.wait_ge(in_seg, 16)
            eng.tensor_copy(seg_f[:, :], seg_i[:, :]).then_inc(seg_made, 1)
            eng.wait_ge(in_attn_w, 32)
            eng.wait_ge(in_consts, 96)
            for j in range(2):
                eng.tensor_scalar(wout[:, :, j, :], wout_n[:, :, :], parity[:, j:j + 1], None, ALU.mult).then_inc(wout_made, 1)

            def statistics(t, p, src, arrived, count, stt, mvt, done, mean, normed):
                if arrived is not None:
                    eng.wait_ge(arrived, count)
                eng.bn_stats(stt[:, p, :], src).then_inc(done, 1)
                eng.wait_ge(done, t + 1)
                eng.sem_inc(dve_begun, 1)
                eng.bn_aggr(mvt[:, p, :], stt[:, p, :]).then_inc(mean, 1)

            def standardise(t, p, src, mvt, rt, dst, ready, used, used_at, done):
                eng.wait_ge(ready, t + 1)
                need(eng, used, used_at)
                eng.tensor_scalar(dst[:, p, :], src, mvt[:, p, 0:1], rt[:, p, :], ALU.subtract, ALU.mult).then_inc(done, 1)

            def mask_a(t, p):
                eng.wait_ge(a_s_ps, t + 1)
                need(eng, a_diff, t - 1)
                eng.tensor_tensor(sm[:, p, 0:512].rearrange("p (r g m) -> p r g m", r=4, g=4),
                                  quad[:, :, 0:P].rearrange("p r (g m) -> p r g m", g=4),
                                  causal[:, None, None, :].to_broadcast([P, 4, 4, L]), ALU.add).then_inc(a_masked, 1)

            def row_max(t, p, width, masked, done):
                eng.wait_ge(masked, t + 1)
                eng.tensor_reduce(mx[:, p, :], sm[:, p, 0:H * width].rearrange("p (h k) -> p h k", h=H),
                                  AX.X, ALU.max).then_inc(done, 1)

            def row_sum(t, p, width, exped, summed, done):
                eng.wait_ge(exped, t + 1)
                eng.tensor_reduce(rs[:, p, :], pe[:, p, 0:H * width].rearrange("p (h k) -> p h k", h=H),
                                  AX.X, ALU.add).then_inc(summed, 1)
                eng.wait_ge(summed, t + 1)
                eng.reciprocal(ri[:, p, :], rs[:, p, :]).then_inc(done, 1)

            def turn_p(t, p):
                eng.wait_ge(a_norm, t + 1)
                need(eng, a_o_ps, t - 1)
                eng.transpose(pt[:, p, 0:512], pn[:, p, 0:512]).then_inc(a_pt, 1)

            def residual_a(t, p):
                eng.wait_ge(a_y_ps, t + 1)
                if live(t - 2):
                    eng.wait_ge(x1_out[p], nth(t - 2, p))
                eng.tensor_tensor(x1[:, p, :], a_y, xall[:, t, :], ALU.add).then_inc(a_x1, 1)

            def step_a(i, p):
                if live(i):
                    mask_a(i, p)
                    row_max(i, p, L, a_masked, a_max)
                if live(i + 2):
                    statistics(i + 2, p, xall[:, i + 2, :], x_in[p], nth(i + 2, p), stat, mv, a_stat, a_mean, a_xh)
                if live(i - 1):
                    residual_a(i - 1, 1 - p)
                if live(i + 2):
                    standardise(i + 2, p, xall[:, i + 2, :], mv, rstd, xh, a_rstd, a_xt_ps, i + 1, a_xh)
                if live(i):
                    row_sum(i, p, L, a_exp, a_sum, a_rec)
                    turn_p(i, p)
                if isinstance(i, int) and i == -2:
                    eng.wait_ge(in_ffn_w, 32)
                    eng.wait_ge(fills, 4)
                    eng.tensor_reduce(gamma[:, :], wff[:, :, :], AX.X, ALU.add, apply_absolute_value=True).then_inc(ternary_steps, 1)

            eng.wait_ge(fills, 4)
            sweep(eng, step_a)

            eng.wait_ge(ternary_steps, 1)
            eng.tensor_scalar(gamma_e[:, :], gamma[:, :], 1.0 / E, Q_EPS, ALU.mult, ALU.add).then_inc(ternary_steps, 1)
            eng.wait_ge(ternary_steps, 2)
            eng.reciprocal(gamma_r[:, :], gamma_e[:, :]).then_inc(ternary_steps, 1)
            eng.wait_ge(ternary_steps, 3)
            for k in range(KT):
                eng.tensor_scalar(wff_n[:, k, :], wff[:, k, :], gamma_r[:, k:k + 1], ROUND, ALU.mult, ALU.add)
                last = eng.tensor_scalar(gamma_d[:, k, :], ident[:, :], gamma[:, k:k + 1], 1.0 / E, ALU.mult, ALU.mult)
            last.then_inc(ternary_steps, 1)
            eng.wait_ge(ternary_steps, 4)
            eng.tensor_scalar(wff[:, :, :], wff_n[:, :, :], ROUND + 1.0, ROUND - 1.0, ALU.min, ALU.max).then_inc(ternary_steps, 1)
            eng.wait_ge(ternary_steps, 5)
            eng.tensor_scalar(wff_q[:, :, :], wff[:, :, :], -ROUND, None, ALU.add).then_inc(ternary_steps, 1)

            def mask_b(t, p):
                eng.wait_ge(b_s_ps, t + 1)
                need(eng, b_diff, t - 1)
                eng.tensor_tensor(sm[:, p, :].rearrange("p (h s k) -> p s h k", s=2, h=HP),
                                  quad[:, 0:2, :].rearrange("p s (h k) -> p s h k", k=N),
                                  window[:, t, None, None, :].to_broadcast([P, 2, HP, N]), ALU.add).then_inc(b_masked, 1)

            def rope_keys(t, p):
                eng.wait_ge(b_kvn, t + 1)
                for dst, s, table in ((kr_a, 0, cos_t), (kr_b, 1, sin_t)):
                    last = eng.tensor_tensor(dst[:, :].rearrange("p (b k) -> p b k", b=BPT),
                                             b_krp[:, s, :].rearrange("p (b k) -> p b k", b=BPT),
                                             table[:, None, :].to_broadcast([P, BPT, N]), ALU.mult)
                last.then_inc(b_kr_ab, 1)
                eng.wait_ge(b_kr_ab, t + 1)
                need(eng, b_s_ps, t - 1)
                eng.tensor_tensor(kr[:, p, :], kr_a[:, :], kr_b[:, :], ALU.add).then_inc(b_kr, 1)

            def rope_queries(t, p, s):
                for part, (dst, table) in enumerate(((qr_a, cos_t), (qr_b, sin_t))):
                    eng.wait_ge(b_proj_ps, 6 * t + 2 * s + part + 3)
                    need(eng, b_qr, 2 * t + s - 1)
                    eng.tensor_tensor(dst[:, s, :].rearrange("p (h q) -> p h q", q=N),
                                      bank[part][:, :].rearrange("p (h q) -> p h q", q=N),
                                      table[:, None, :].to_broadcast([P, HP, N]), ALU.mult).then_inc(b_rope, 1)

            def residual_b(t, p):
                eng.wait_ge(b_y_ps, t + 1)
                need(eng, c_x2b, t - 1)
                eng.tensor_tensor(x2[:, p, :], b_y, xall[:, t, :], ALU.add).then_inc(c_x2, 1)

            def largest(t, p):
                eng.wait_ge(c_h, t + 1)
                eng.tensor_reduce(mh[:, p, :], h3[:, p, :], AX.X, ALU.max, apply_absolute_value=True).then_inc(c_mh, 1)

            def quantise(t, p):
                eng.wait_ge(c_rq, t + 1)
                eng.wait_ge(c_mh, t + 1)
                steps = 6 * t
                eng.tensor_scalar(xs[:, p, :], mh[:, p, :], rq[:, p, :], 1.0 / QB, ALU.mult, ALU.mult).then_inc(c_scale, 1)
                eng.wait_ge(c_scale, steps + 1)
                eng.tensor_scalar(xse[:, p, :], xs[:, p, :], Q_EPS, None, ALU.add).then_inc(c_scale, 1)
                eng.wait_ge(c_scale, steps + 2)
                eng.reciprocal(xsr[:, p, :], xse[:, p, :]).then_inc(c_scale, 1)
                eng.wait_ge(c_scale, steps + 3)
                eng.tensor_scalar(hc[:, p, :], h3[:, p, :], rq[:, p, :], None, ALU.mult).then_inc(c_scale, 1)
                eng.wait_ge(c_scale, steps + 4)
                eng.tensor_scalar(hr[:, p, :], hc[:, p, :], xsr[:, p, :], ROUND, ALU.mult, ALU.add).then_inc(c_scale, 1)
                eng.wait_ge(c_scale, steps + 5)
                eng.tensor_scalar(hc[:, p, :], hr[:, p, :], ROUND + QB, ROUND - QB, ALU.min, ALU.max).then_inc(c_scale, 1)
                eng.wait_ge(c_scale, steps + 6)
                need(eng, c_t_ps, t - 1)
                eng.tensor_scalar(xq[:, p, :], hc[:, p, :], -ROUND, None, ALU.add).then_inc(c_xq, 1)

            def finish(t, p):
                eng.wait_ge(c_y_ps, t + 1)
                eng.scalar_tensor_tensor(ffs[:, p, :], c_yp, xs[:, p, :], gamma_b[:, :], ALU.mult, ALU.mult).then_inc(c_ffs, 1)
                eng.wait_ge(c_ffs, t + 1)
                eng.wait_ge(c_x2b, t + 1)
                if live(t - 2):
                    eng.wait_ge(out_done[p], nth(t - 2, p))
                eng.tensor_tensor(res[:, p, :], ffs[:, p, :], x2b[:, p, :], ALU.add).then_inc(c_out, 1)

            def step_b(i, p):
                if live(i - 3):
                    finish(i - 3, 1 - p)
                if live(i - 2):
                    residual_b(i - 2, p)
                    statistics(i - 2, p, x2[:, p, :], c_x2, i - 1, stat3, mv3, c_stat, c_mean, c_h)
                    standardise(i - 2, p, x2[:, p, :], mv3, rstd3, h3, c_rstd, c_ssq, i - 3, c_h)
                    largest(i - 2, p)
                if live(i):
                    mask_b(i, p)
                    row_max(i, p, N, b_masked, b_max)
                if live(i + 2):
                    statistics(i + 2, p, xall[:, i + 2, :], x1_in[p], nth(i + 2, p), stat, mv, b_stat, b_mean, b_xh)
                if live(i - 2):
                    quantise(i - 2, p)
                if live(i + 2):
                    standardise(i + 2, p, xall[:, i + 2, :], mv, rstd, xh, b_rstd, b_xt_ps, i + 1, b_xh)
                if live(i + 1):
                    rope_queries(i + 1, 1 - p, 0)
                    rope_queries(i + 1, 1 - p, 1)
                    rope_keys(i + 1, 1 - p)
                if live(i):
                    row_sum(i, p, N, b_exp, b_sum, b_rec)

            eng.wait_ge(products, 11)
            eng.wait_ge(window_steps, 4)
            sweep(eng, step_b)


def swap_halves(w, heads):
    k = w.shape[0]
    return np.ascontiguousarray(w.reshape(k, heads, 2, R // 2)[:, :, ::-1, :].reshape(k, heads * R))


def shape_constants():
    half = R // 2
    inv_freq = (np.float32(1.0) / np.power(np.float32(10000.0), np.arange(half, dtype=np.float32) / np.float32(half))).astype(np.float32)
    ang = (np.arange(N, dtype=np.float32)[:, None] * inv_freq).astype(np.float32)
    cos, sin = np.cos(ang).T, np.sin(ang).T
    row = np.arange(P)
    return {
        "ident_c": np.eye(P, dtype=np.float32),
        "causal_c": np.where(np.arange(L)[None, :] <= (row % L)[:, None], 0.0, NEG).astype(np.float32),
        "parity_c": ((row // DH % 2)[:, None] == np.arange(2)[None, :]).astype(np.float32),
        "cos_c": np.concatenate([cos, cos, cos, cos]).astype(np.float32),
        "sin_c": np.concatenate([-sin, sin, -sin, sin]).astype(np.float32),
        "kidx_c": np.tile(np.arange(N, dtype=np.float32), (P, 1)),
    }


def kernel(x, ctx_2048, itok_BxS_0_1023, L0_attn_weight_qkv, L0_attn_weight_out, L0_xattn_W_kvc, L0_xattn_W_dq,
           L0_xattn_W_uq, L0_xattn_W_qr, L0_xattn_W_uk, L0_xattn_W_kr, L0_xattn_W_uv, L0_xattn_W_o,
           L0_ffn_weight, L0_ffn_bias):
    import concourse.bacc as _bacc
    from concourse.bass_utils import run_bass_kernel_spmd as _run

    lay = np.ascontiguousarray
    a = {
        "x": lay(x),
        "ctx_t": lay(np.asarray(ctx_2048).reshape(NT, P, KT, P).transpose(0, 3, 2, 1).reshape(NT, P, KT * P)),
        "seg": lay(np.asarray(itok_BxS_0_1023).reshape(NT, P).T),
        "w_qkv_t": lay(np.asarray(L0_attn_weight_qkv).T),
        "w_out_t": lay(np.asarray(L0_attn_weight_out).T),
        "w_kvc": lay(L0_xattn_W_kvc),
        "w_kvc_t": lay(np.asarray(L0_xattn_W_kvc).T),
        "w_dq": lay(L0_xattn_W_dq),
        "w_uq_t": lay(np.asarray(L0_xattn_W_uq).reshape(QC, H, HD).transpose(2, 1, 0)),
        "w_qr": lay(L0_xattn_W_qr),
        "w_qr_s": swap_halves(np.asarray(L0_xattn_W_qr), H),
        "w_uk_t": lay(np.asarray(L0_xattn_W_uk).reshape(KVC, H, HD).transpose(2, 1, 0)),
        "w_kr": lay(L0_xattn_W_kr),
        "w_kr_s": swap_halves(np.asarray(L0_xattn_W_kr), 1),
        "w_uv_t": lay(np.asarray(L0_xattn_W_uv).reshape(KVC, H, HD).transpose(2, 1, 0)),
        "w_o": lay(np.asarray(L0_xattn_W_o).reshape(H, HD, E).transpose(1, 0, 2)),
        "w_ff": lay(L0_ffn_weight),
        "b_ff": lay(np.asarray(L0_ffn_bias).reshape(1, E)),
    }
    a.update(shape_constants())
    nc = _bacc.Bacc("TRN2", target_bir_lowering=False, num_devices=1)
    args = {n: nc.dram_tensor(n, v.shape, mybir.dt.from_np(v.dtype), kind="ExternalInput").ap() for n, v in a.items()}
    x1_dram = nc.dram_tensor("x1_dram", (L, N, E), F32, kind="Internal").ap()
    out = nc.dram_tensor("out", (L, N, E), F32, kind="ExternalOutput").ap()
    decoder_layer(nc, x1_dram=x1_dram, out=out, **args)
    return _run(nc, [a], core_ids=[0]).results[0]["out"]
```

```python
from contextlib import ExitStack

import numpy as np

import concourse.bass as bass
from concourse import mybir

P = 128
E = 256
KT = E // P
NT = 16
L, N = 32, 64
H = 16
DH = 16
NPT = P // L
BPT = P // N
HP = H // 2
KVC, QC, R, HD = 64, 96, 64, 128
LOOKBACK = 8
NEG = -1e30
LN_EPS = 1e-5
Q_EPS = 1e-8
QB = 127.0
ROUND = 12582912.0
SELF_SCALE = DH ** -0.5
CROSS_SCALE = float(np.float32(1.0) / np.sqrt(HD + R).astype(np.float32))

ALU = mybir.AluOpType
ACT = mybir.ActivationFunctionType
AX = mybir.AxisListType
F32 = mybir.dt.float32
BF16 = mybir.dt.bfloat16
I32 = mybir.dt.int32


def need(eng, sem, count):
    if not isinstance(count, int) or count > 0:
        eng.wait_ge(sem, count)


def live(t):
    return not isinstance(t, int) or 0 <= t < NT


def upto(t):
    return min(t, NT) if isinstance(t, int) else t


def nth(t, p):
    return 8 * (t - p + 2)


def sweep(eng, step, first):
    for i in range(-2, 2 * first):
        step(i, i % 2)
    with eng.Fori(first, NT // 2 - 1) as j:
        for p in range(2):
            step(2 * j + p, p)
    for i in range(NT - 2, NT + 4):
        step(i, i % 2)


def decoder_layer(nc, x, ctx_t, seg, w_qkv_t, w_out_t, w_kvc, w_kvc_t, w_dq, w_uq_t, w_qr, w_qr_s,
                  w_uk_t, w_kr, w_kr_s, w_uv_t, w_o, w_ff, b_ff, ident_c, causal_c, parity_c,
                  cos_c, sin_c, kidx_c, x1_dram, out):
    with ExitStack() as ctx:
        def sb(name, shape, dt=F32):
            return ctx.enter_context(nc.sbuf_tensor(name, shape, dt))

        def sem(name):
            return ctx.enter_context(nc.semaphore(name))

        bank = [ctx.enter_context(nc.psum_tensor(f"bank{i}", [P, 512], F32)) for i in range(4)]
        quad = ctx.enter_context(nc.psum_tensor("quad", [P, 4, 512], F32))

        ident = sb("ident", [P, P])
        ident_b = sb("ident_b", [P, P], BF16)
        ones = sb("ones", [P, P])
        neg_half = sb("neg_half", [P, 1])
        ln_eps = sb("ln_eps", [P, 1])
        causal = sb("causal", [P, L])
        parity = sb("parity", [P, 2])
        cos_t = sb("cos_t", [P, N])
        sin_t = sb("sin_t", [P, N])
        kidx = sb("kidx", [P, N])
        seg_i = sb("seg_i", [P, NT, BPT], I32)
        seg_f = sb("seg_f", [P, NT, BPT])
        window = sb("window", [P, NT, P])
        window4 = window[:, :, :].rearrange("p t (b k) -> p t b k", b=BPT)
        wqkv = sb("wqkv", [P, KT, 3 * E])
        wout_n = sb("wout_n", [P, KT, E])
        wout = sb("wout", [P, KT, 2, E])
        wkvc2 = sb("wkvc2", [P, KT, 2, KVC])
        wkvc_t = sb("wkvc_t", [KVC, E])
        wdq = sb("wdq", [P, KT, QC])
        wuq_t = sb("wuq_t", [P, H, QC])
        st = sb("st", [P, 2, 1024])
        wuk_t = st[:, 0, :].rearrange("p (h c) -> p h c", h=H)
        wuv_t = st[:, 1, :].rearrange("p (h c) -> p h c", h=H)
        wqr = sb("wqr", [QC, H * R])
        wqr_s = sb("wqr_s", [QC, H * R])
        wkr = sb("wkr", [KVC, R])
        wkr_s = sb("wkr_s", [KVC, R])
        wkr2 = sb("wkr2", [P, KT, 2, R])
        wkr2_s = sb("wkr2_s", [P, KT, 2, R])
        qn_qr = sb("qn_qr", [P, 2, 2, HP, P])
        qn, qr = qn_qr[:, 0, :, :, :], qn_qr[:, 1, :, :, :]
        wo = qn_qr[:, :, :, :, :].rearrange("p a b h t -> p (a b h t)").rearrange("p (h e) -> p h e", h=H)
        wqn = sb("wqn", [QC, HP, 2 * KVC])
        wvo = sb("wvo", [P, HP, E])
        wff = sb("wff", [P, KT, E])
        wff_n = sb("wff_n", [P, KT, E])
        wff_q = sb("wff_q", [P, KT, E], BF16)
        wff_t = sb("wff_t", [P, KT, E], BF16)
        gamma = sb("gamma", [P, KT])
        gamma_e = sb("gamma_e", [P, KT])
        gamma_r = sb("gamma_r", [P, KT])
        gamma_d = sb("gamma_d", [P, KT, P])
        gamma_b = sb("gamma_b", [P, E])
        bias_b = sb("bias_b", [P, E])

        xall = sb("xall", [P, NT, E])
        stat = sb("stat", [P, 2, 6])
        mv = sb("mv", [P, 2, 2])
        ve = sb("ve", [P, 2, 1])
        rstd = sb("rstd", [P, 2, 1])
        xh = sb("xh", [P, 2, E])
        xt = sb("xt", [P, 2, KT, P])
        qt = sb("qt", [P, 2, 2, P])
        kx = sb("kx", [P, 2, 2, 2, P])
        vs = sb("vs", [P, 2, E])
        sm = sb("sm", [P, 2, 1024])
        sd = sb("sd", [P, 2, 1024])
        pe = sb("pe", [P, 2, 1024])
        pn = sb("pn", [P, 2, 1024])
        mx = sb("mx", [P, 2, H])
        rs = sb("rs", [P, 2, H])
        ri = sb("ri", [P, 2, H])
        pt = sb("pt", [P, 2, 1024])
        ot = sb("ot", [P, 2, 4, P])
        x1 = sb("x1", [P, 2, E])
        ctxt = sb("ctxt", [P, 2, KT, P])
        kn = sb("kn", [P, 2, P])
        kr = sb("kr", [P, 2, P])
        kr_a = sb("kr_a", [P, P])
        kr_b = sb("kr_b", [P, P])
        kvn = sb("kvn", [P, 2, KVC])
        qct = sb("qct", [QC, 2, P])
        qr_a = sb("qr_a", [P, 2, 512])
        qr_b = sb("qr_b", [P, 2, 512])
        ctxo = sb("ctxo", [P, 2, HP, P])
        window2 = ctxo[:, :, :, :].rearrange("p a h t -> p (a h) t")
        x2 = sb("x2", [P, 2, E])
        x2b = sb("x2b", [P, 2, E])
        stat3 = sb("stat3", [P, 2, 6])
        mv3 = sb("mv3", [P, 2, 2])
        ve3 = sb("ve3", [P, 2, 1])
        rstd3 = sb("rstd3", [P, 2, 1])
        h3 = sb("h3", [P, 2, E])
        hsq = sb("hsq", [P, 2, E])
        ssq = sb("ssq", [P, 2, 1])
        mh = sb("mh", [P, 2, 1])
        vq = sb("vq", [P, 2, 1])
        rq = sb("rq", [P, 2, 1])
        xs = sb("xs", [P, 2, 1])
        xse = sb("xse", [P, 2, 1])
        xsr = sb("xsr", [P, 2, 1])
        fq = sb("fq", [P, 2, 1])
        hr = sb("hr", [P, 2, E])
        hc = sb("hc", [P, 2, E])
        xq = sb("xq", [P, 2, E], BF16)
        xqt = sb("xqt", [P, 2, KT, P], BF16)
        ffs = sb("ffs", [P, 2, E])
        res = sb("res", [P, 2, E])

        in_ident, in_wqkv, in_masks, in_wout, in_window, in_cross_w, in_ffn_w = (sem(s) for s in (
            "in_ident", "in_wqkv", "in_masks", "in_wout", "in_window", "in_cross_w", "in_ffn_w"))
        fills = sem("fills")
        pe_begun, dve_begun = sem("pe_begun"), sem("dve_begun")
        ident_b_made, seg_made, wout_made, window_steps, ternary_steps, products_ps, products = (sem(s) for s in (
            "ident_b_made", "seg_made", "wout_made", "window_steps", "ternary_steps", "products_ps", "products"))
        x_in = [sem(f"x_in{p}") for p in range(2)]
        x1_out = [sem(f"x1_out{p}") for p in range(2)]
        x1_in = [sem(f"x1_in{p}") for p in range(2)]
        ctx_in = [sem(f"ctx_in{p}") for p in range(2)]
        out_done = [sem(f"out_done{p}") for p in range(2)]
        a_stat, a_mean, a_var, a_rstd, a_xh = (sem(s) for s in ("a_stat", "a_mean", "a_var", "a_rstd", "a_xh"))
        a_xt_ps, a_xt, a_qk_ps, a_qk, a_v_ps, a_v = (sem(s) for s in (
            "a_xt_ps", "a_xt", "a_qk_ps", "a_qk", "a_v_ps", "a_v"))
        a_s_ps, a_masked, a_max, a_diff, a_exp, a_sum, a_rec, a_norm, a_pt = (sem(s) for s in (
            "a_s_ps", "a_masked", "a_max", "a_diff", "a_exp", "a_sum", "a_rec", "a_norm", "a_pt"))
        a_o_ps, a_o, a_y_ps, a_x1 = (sem(s) for s in ("a_o_ps", "a_o", "a_y_ps", "a_x1"))
        b_stat, b_mean, b_var, b_rstd, b_xh = (sem(s) for s in ("b_stat", "b_mean", "b_var", "b_rstd", "b_xh"))
        b_xt_ps, b_xt, b_qc_ps, b_qc = (sem(s) for s in ("b_xt_ps", "b_xt", "b_qc_ps", "b_qc"))
        b_k_ps, b_kn, b_kr_ab, b_kr, b_kvn_ps, b_kvn = (sem(s) for s in (
            "b_k_ps", "b_kn", "b_kr_ab", "b_kr", "b_kvn_ps", "b_kvn"))
        b_proj_ps, b_qn, b_rope, b_qr = (sem(s) for s in ("b_proj_ps", "b_qn", "b_rope", "b_qr"))
        b_st_ps, b_st, b_s_ps, b_masked, b_max, b_diff, b_exp, b_sum, b_rec, b_norm = (sem(s) for s in (
            "b_st_ps", "b_st", "b_s_ps", "b_masked", "b_max", "b_diff", "b_exp", "b_sum", "b_rec", "b_norm"))
        b_pt_ps, b_pt, b_c_ps, b_c, b_y_ps = (sem(s) for s in ("b_pt_ps", "b_pt", "b_c_ps", "b_c", "b_y_ps"))
        c_x2, c_x2b, c_stat, c_mean, c_var, c_rstd, c_h, c_ssq, c_mh = (sem(s) for s in (
            "c_x2", "c_x2b", "c_stat", "c_mean", "c_var", "c_rstd", "c_h", "c_ssq", "c_mh"))
        c_vq, c_rq, c_scale, c_xq = (sem(s) for s in ("c_vq", "c_rq", "c_scale", "c_xq"))
        c_t_ps, c_t, c_y_ps, c_ffs, c_out = (sem(s) for s in ("c_t_ps", "c_t", "c_y_ps", "c_ffs", "c_out"))

        x_cols = x.rearrange("l (t n) e -> t n l e", n=NPT)
        x1_cols = x1_dram.rearrange("l (t n) e -> t n l e", n=NPT)
        x1_rows = x1_dram.rearrange("(t b) n e -> t (b n) e", b=BPT)
        out_rows = out.rearrange("(t b) n e -> t (b n) e", b=BPT)

        a_t = bank[0][:, 0:E].rearrange("p (k t) -> p k t", k=KT)
        a_qkp = bank[1][:, :].rearrange("p (f t) -> p f t", f=4)
        a_vp = bank[2][:, 0:E]
        a_y = bank[3][:, 0:E]
        b_t = bank[2][:, 0:E].rearrange("p (k t) -> p k t", k=KT)
        b_qcp = bank[2][0:QC, E:E + P]
        b_y = bank[2][:, 0:E]
        b_knp = bank[3][:, 0:P]
        b_krp = bank[3][:, P:3 * P].rearrange("p (s t) -> p s t", s=2)
        b_kvnp = bank[3][:, 3 * P:3 * P + KVC]
        c_tp = bank[3][:, 0:P].bitcast(BF16).rearrange("p (k t) -> p k t", k=KT)
        c_yp = bank[3][:, 0:E]

        block = ctx.enter_context(nc.Block())

        @block.sync
        def _(eng):
            def load_x(t, p):
                need(eng, a_stat, t - 1)
                eng.dma_start(xall[:, t, :], x_cols[t]).then_inc(x_in[p], 16)

            load_x(0, 0)
            load_x(1, 1)
            eng.dma_start(seg_i[:, :, :], seg).then_inc(in_window, 16)
            eng.dma_start(kidx[:, :], kidx_c).then_inc(in_window, 16)
            eng.dma_start(wff[:, :, :], w_ff.rearrange("(k p) f -> p k f", p=P)).then_inc(in_ffn_w, 16)
            eng.dma_start(bias_b[:, :], b_ff.to_broadcast([P, E])).then_inc(in_ffn_w, 16)

            def load_cross_weights():
                eng.dma_start(cos_t[:, :], cos_c).then_inc(in_cross_w, 16)
                eng.dma_start(sin_t[:, :], sin_c).then_inc(in_cross_w, 16)
                for d in range(2):
                    eng.dma_start(wkvc2[:, :, d, :], w_kvc.rearrange("(k p) c -> p k c", p=P)).then_inc(in_cross_w, 16)
                for dst, src in ((wkvc_t, w_kvc_t), (wqr, w_qr), (wqr_s, w_qr_s), (wkr, w_kr), (wkr_s, w_kr_s)):
                    eng.dma_start(dst[:, :], src).then_inc(in_cross_w, 16)
                eng.dma_start(wdq[:, :, :], w_dq.rearrange("(k p) c -> p k c", p=P)).then_inc(in_cross_w, 16)
                for dst, src in ((wuq_t[:, :, :], w_uq_t), (wuk_t, w_uk_t), (wuv_t, w_uv_t), (wo, w_o)):
                    eng.dma_start(dst, src).then_inc(in_cross_w, 16)

            def store_x1(t, p):
                eng.wait_ge(a_x1, t + 1)
                eng.dma_start(x1_cols[t], x1[:, p, :]).then_inc(x1_out[p], 16)

            def step_a(i, p):
                if live(i + 2) and not (isinstance(i, int) and i < 0):
                    load_x(i + 2, p)
                if isinstance(i, int) and i == 1:
                    load_cross_weights()
                if live(i - 1):
                    store_x1(i - 1, 1 - p)

            sweep(eng, step_a, 2)

            for p in range(2):
                eng.wait_ge(x1_out[p], 16 * NT // 2)

            def load_b(t, p):
                need(eng, b_stat, t - 1)
                eng.dma_start(xall[:, t, :], x1_rows[t]).then_inc(x1_in[p], 16)
                need(eng, b_kvn_ps, t - 1)
                eng.dma_start(ctxt[:, p, :, :], ctx_t[t].rearrange("p (k t) -> p k t", k=KT)).then_inc(ctx_in[p], 16)

            def store_out(t, p):
                eng.wait_ge(c_out, t + 1)
                eng.dma_start(out_rows[t], res[:, p, :]).then_inc(out_done[p], 16)

            def step_b(i, p):
                if live(i + 2):
                    load_b(i + 2, p)
                if live(i - 3):
                    store_out(i - 3, 1 - p)

            sweep(eng, step_b, 3)
            for p in range(2):
                eng.wait_ge(out_done[p], 16 * NT // 2)

        @block.gpsimd
        def _(eng):
            eng.memset(ones[:, :], 1.0).then_inc(fills, 1)
            eng.memset(neg_half[:, :], -0.5).then_inc(fills, 1)
            eng.memset(ln_eps[:, :], LN_EPS).then_inc(fills, 1)
            eng.wait_ge(fills, 3)
            def make_window(n):
                if n == 0:
                    eng.wait_ge(seg_made, 1)
                    eng.tensor_tensor(window4, kidx[:, None, None, :].to_broadcast([P, NT, BPT, N]),
                                      seg_f[:, :, :, None].to_broadcast([P, NT, BPT, N]), ALU.subtract).then_inc(window_steps, 1)
                    return
                eng.wait_ge(window_steps, n)
                if n == 1:
                    eng.tensor_scalar(window2, window[:, :, :], 0.0, NEG, ALU.is_gt, ALU.mult).then_inc(window_steps, 1)
                if n == 2:
                    eng.tensor_scalar(window[:, :, :], window[:, :, :], -float(LOOKBACK), NEG, ALU.is_lt, ALU.mult).then_inc(window_steps, 1)
                if n == 3:
                    eng.tensor_tensor(window[:, :, :], window[:, :, :], window2, ALU.add).then_inc(window_steps, 1)

            def inverse_root(t, p, mean, mvt, vet, var, rt, done):
                eng.wait_ge(mean, t + 1)
                eng.tensor_tensor(vet[:, p, :], mvt[:, p, 1:2], ln_eps[:, :], ALU.add).then_inc(var, 1)
                eng.wait_ge(var, t + 1)
                eng.tensor_tensor(rt[:, p, :], vet[:, p, :], neg_half[:, :], ALU.pow).then_inc(done, 1)

            def submax(t, p, width, maxed, exped, done):
                eng.wait_ge(maxed, t + 1)
                need(eng, exped, t - 1)
                m = H * width
                eng.tensor_tensor(sd[:, p, 0:m].rearrange("p (h k) -> p h k", h=H),
                                  sm[:, p, 0:m].rearrange("p (h k) -> p h k", h=H),
                                  mx[:, p, :, None].to_broadcast([P, H, width]), ALU.subtract).then_inc(done, 1)

            def normalise(t, p, width, recip, used, uses, done):
                eng.wait_ge(recip, t + 1)
                need(eng, used, uses * (t - 1))
                m = H * width
                eng.tensor_tensor(pn[:, p, 0:m].rearrange("p (h k) -> p h k", h=H),
                                  pe[:, p, 0:m].rearrange("p (h k) -> p h k", h=H),
                                  ri[:, p, :, None].to_broadcast([P, H, width]), ALU.mult).then_inc(done, 1)

            def step_a(i, p):
                if live(i):
                    submax(i, p, L, a_max, a_exp, a_diff)
                if live(i + 2):
                    inverse_root(i + 2, p, a_mean, mv, ve, a_var, rstd, a_rstd)
                if live(i):
                    normalise(i, p, L, a_rec, a_pt, 1, a_norm)
                if isinstance(i, int) and -1 <= i <= 2:
                    make_window(i + 1)

            sweep(eng, step_a, 2)

            def add_rope(t, p, s):
                eng.wait_ge(b_rope, 4 * t + 2 * s + 2)
                need(eng, b_st_ps, t - 1)
                eng.tensor_tensor(qr[:, p, 4 * s:4 * s + 4, :].rearrange("p h t -> p (h t)"), qr_a[:, s, :], qr_b[:, s, :], ALU.add).then_inc(b_qr, 1)

            def biased(t, p):
                eng.wait_ge(c_x2, t + 1)
                need(eng, c_out, t - 1)
                eng.tensor_tensor(x2b[:, p, :], x2[:, p, :], bias_b[:, :], ALU.add).then_inc(c_x2b, 1)

            def inverse_rms(t, p):
                need(eng, c_xq, t - 1)
                eng.wait_ge(c_vq, t + 1)
                eng.tensor_tensor(rq[:, p, :], vq[:, p, :], neg_half[:, :], ALU.pow).then_inc(c_rq, 1)

            def step_b(i, p):
                if live(i - 2):
                    inverse_root(i - 2, p, c_mean, mv3, ve3, c_var, rstd3, c_rstd)
                    biased(i - 2, p)
                    inverse_rms(i - 2, p)
                if live(i):
                    submax(i, p, N, b_max, b_exp, b_diff)
                if live(i + 2):
                    inverse_root(i + 2, p, b_mean, mv, ve, b_var, rstd, b_rstd)
                if live(i + 1):
                    add_rope(i + 1, 1 - p, 0)
                    add_rope(i + 1, 1 - p, 1)
                if live(i):
                    normalise(i, p, N, b_rec, b_pt_ps, 2, b_norm)

            eng.wait_ge(in_ffn_w, 32)
            sweep(eng, step_b, 3)

        @block.scalar
        def _(eng):
            eng.dma_start(ident[:, :], ident_c).then_inc(in_ident, 16)
            for k in range(KT):
                eng.dma_start(wqkv[:, k, :], w_qkv_t[k * P:(k + 1) * P, :]).then_inc(in_wqkv, 16)
            eng.dma_start(parity[:, :], parity_c).then_inc(in_masks, 16)
            eng.dma_start(causal[:, :], causal_c).then_inc(in_masks, 16)
            eng.dma_start(wout_n[:, :, :], w_out_t.rearrange("(k p) f -> p k f", p=P)).then_inc(in_wout, 16)
            eng.wait_ge(in_ident, 16)
            eng.wait_ge(in_masks, 32)
            eng.activation(ident_b[:, :], ident[:, :], ACT.Copy).then_inc(ident_b_made, 1)

            def x_t(t, p, made, used, done, src):
                eng.wait_ge(made, t + 1)
                need(eng, used, t - 1)
                eng.activation(xt[:, p, :, :], src, ACT.Copy).then_inc(done, 1)

            def heads_out(t, p):
                eng.wait_ge(a_o_ps, t + 1)
                need(eng, a_y_ps, t - 1)
                eng.activation(ot[:, p, :, :].rearrange("p g (n l) -> p n g l", n=NPT),
                               quad[:, :, 0:P].rearrange("p n (g l) -> p n g l", g=4), ACT.Copy).then_inc(a_o, 1)

            def exps(t, p, width, scale, diff, normed, done):
                eng.wait_ge(diff, t + 1)
                need(eng, normed, t - 1)
                eng.activation(pe[:, p, 0:H * width], sd[:, p, 0:H * width], ACT.Exp, scale=scale).then_inc(done, 1)

            def queries_keys(t, p):
                eng.wait_ge(a_qk_ps, t + 1)
                need(eng, a_s_ps, t - 1)
                eng.activation(qt[:, p, :, :], a_qkp[:, 0:2, :], ACT.Copy)
                for j in range(2):
                    last = eng.activation(kx[:, p, :, j, :], a_qkp[:, 2:4, :], ACT.Copy, scale=parity[:, j:j + 1])
                last.then_inc(a_qk, 1)

            def values(t, p):
                eng.wait_ge(a_v_ps, t + 1)
                need(eng, a_o_ps, t - 1)
                eng.activation(vs[:, p, :], a_vp, ACT.Copy).then_inc(a_v, 1)

            def step_a(i, p):
                if live(i + 1):
                    x_t(i + 1, 1 - p, a_xt_ps, a_v_ps, a_xt, a_t)
                if live(i):
                    exps(i, p, L, SELF_SCALE, a_diff, a_norm, a_exp)
                if live(i - 1):
                    heads_out(i - 1, 1 - p)
                if live(i + 1):
                    queries_keys(i + 1, 1 - p)
                if live(i + 1):
                    values(i + 1, 1 - p)

            sweep(eng, step_a, 2)

            for g in range(4):
                eng.wait_ge(products_ps, 2 * g + 1)
                eng.activation(wqn[:, 2 * g:2 * g + 2, :].rearrange("q h c -> q (h c)"), bank[0][0:QC, 0:4 * KVC], ACT.Copy).then_inc(products, 1)
                eng.wait_ge(products_ps, 2 * g + 2)
                eng.activation(wvo[:, 2 * g:2 * g + 2, :].rearrange("q h c -> q (h c)"), bank[1][:, :], ACT.Copy).then_inc(products, 1)
            eng.wait_ge(products_ps, 9)
            for k in range(KT):
                for d in range(2):
                    eng.activation(wkr2[:, k, d, :], bank[2][:, k * R:(k + 1) * R], ACT.Copy)
                    last = eng.activation(wkr2_s[:, k, d, :], bank[2][:, (2 + k) * R:(3 + k) * R], ACT.Copy)
            last.then_inc(products, 1)
            eng.wait_ge(products_ps, 10)
            eng.activation(wff_t[:, :, :], quad[:, 0, 0:E].bitcast(BF16).rearrange("p (k n) -> p k n", k=KT), ACT.Copy).then_inc(products, 1)
            eng.wait_ge(products_ps, 11)
            eng.activation(gamma_b[:, :], quad[:, 1, 0:E], ACT.Copy).then_inc(products, 1)

            def keys_nope(t, p):
                eng.wait_ge(b_k_ps, t + 1)
                need(eng, b_st_ps, t - 1)
                eng.activation(kn[:, p, :], b_knp, ACT.Copy).then_inc(b_kn, 1)

            def keys_rows(t, p):
                eng.wait_ge(b_kvn_ps, t + 1)
                need(eng, b_c_ps, t - 1)
                eng.activation(kvn[:, p, :], b_kvnp, ACT.Copy).then_inc(b_kvn, 1)

            def scores_t(t, p):
                eng.wait_ge(b_st_ps, t + 1)
                need(eng, b_s_ps, t - 1)
                eng.activation(st[:, p, :].rearrange("p (h s q) -> p s h q", h=HP, s=2),
                               quad[:, 0:2, :].rearrange("p s (h q) -> p s h q", h=HP), ACT.Copy).then_inc(b_st, 1)

            def p_t(t, p, s):
                eng.wait_ge(b_pt_ps, 2 * t + s + 1)
                need(eng, b_c_ps, t - 1)
                eng.activation(pt[:, p, 512 * s:512 * s + 512], quad[:, s, :], ACT.Copy).then_inc(b_pt, 1)

            def q_c(t, p):
                eng.wait_ge(b_qc_ps, t + 1)
                need(eng, b_proj_ps, 6 * (t - 1))
                eng.activation(qct[:, p, :], b_qcp, ACT.Copy).then_inc(b_qc, 1)

            def contexts(t, p):
                eng.wait_ge(b_c_ps, t + 1)
                need(eng, b_y_ps, t - 1)
                eng.activation(ctxo[:, p, :, :].rearrange("p h (b q) -> p b h q", b=BPT),
                               quad[:, 2:4, :].rearrange("p b (h q) -> p b h q", h=HP), ACT.Copy).then_inc(b_c, 1)

            def queries_nope(t, p, s):
                eng.wait_ge(b_proj_ps, 6 * t + s + 1)
                need(eng, b_st_ps, t - 1)
                eng.activation(qn[:, p, 4 * s:4 * s + 4, :].rearrange("p h t -> p (h t)"), bank[s][:, :],
                               ACT.Copy).then_inc(b_qn, 1)

            def squares(t, p):
                eng.wait_ge(c_h, t + 1)
                need(eng, c_vq, t - 1)
                eng.activation(hsq[:, p, :], h3[:, p, :], ACT.Square, accum_out=ssq[:, p, :]).then_inc(c_ssq, 1)
                eng.wait_ge(c_ssq, t + 1)
                need(eng, c_rq, t - 1)
                eng.activation(vq[:, p, :], ssq[:, p, :], ACT.Copy, scale=1.0 / E, bias=Q_EPS).then_inc(c_vq, 1)

            def x_q_t(t, p):
                eng.wait_ge(c_t_ps, t + 1)
                need(eng, c_y_ps, t - 1)
                eng.activation(xqt[:, p, :, :], c_tp, ACT.Copy).then_inc(c_t, 1)

            def step_b(i, p):
                if live(i - 2):
                    squares(i - 2, p)
                if live(i):
                    scores_t(i, p)
                if live(i + 1):
                    x_t(i + 1, 1 - p, b_xt_ps, b_qc_ps, b_xt, b_t)
                    keys_nope(i + 1, 1 - p)
                if live(i):
                    keys_rows(i, p)
                if live(i - 1):
                    p_t(i - 1, 1 - p, 0)
                    p_t(i - 1, 1 - p, 1)
                if live(i + 1):
                    q_c(i + 1, 1 - p)
                    queries_nope(i + 1, 1 - p, 0)
                    queries_nope(i + 1, 1 - p, 1)
                if live(i - 1):
                    contexts(i - 1, 1 - p)
                if live(i):
                    exps(i, p, N, CROSS_SCALE, b_diff, b_norm, b_exp)
                if live(i - 2):
                    x_q_t(i - 2, p)

            sweep(eng, step_b, 3)

        @block.tensor
        def _(eng):
            def transpose_x(t, p, ready, freed, free_at, dst, done):
                eng.wait_ge(ready, t + 1)
                need(eng, freed, free_at)
                for k in range(KT):
                    last = eng.transpose(dst[:, k, :], xh[:, p, k * P:(k + 1) * P], ident[:, :])
                last.then_inc(done, 1)

            def qkv(t, p):
                eng.wait_ge(a_xt, t + 1)
                need(eng, a_qk, t)
                if isinstance(t, int) and t == 0:
                    eng.wait_ge(in_wqkv, 32)
                for f in range(4):
                    for k in range(KT):
                        last = eng.matmul(a_qkp[:, f, :], wqkv[:, k, f * P:(f + 1) * P], xt[:, p, k, :],
                                          start=k == 0, stop=k == KT - 1)
                last.then_inc(a_qk_ps, 1)
                need(eng, a_v, t)
                for k in range(KT):
                    last = eng.matmul(a_vp, xt[:, p, k, :], wqkv[:, k, 2 * E:3 * E], start=k == 0, stop=k == KT - 1)
                last.then_inc(a_v_ps, 1)

            def scores_a(t, p):
                eng.wait_ge(a_qk, t + 1)
                need(eng, a_masked, t)
                need(eng, a_o, t - 1)
                eng.sem_inc(pe_begun, 1)
                for g in range(2):
                    for n in range(NPT):
                        for r in range(4):
                            last = eng.matmul(quad[32 * n:32 * n + 32, r, g * 64:g * 64 + 64],
                                              qt[32 * r:32 * r + 32, p, g, 32 * n:32 * n + 32],
                                              kx[32 * r:32 * r + 32, p, g, :, 32 * n:32 * n + 32],
                                              start=True, stop=True)
                last.then_inc(a_s_ps, 1)

            def weigh_a(t, p):
                eng.wait_ge(a_masked, upto(t + 2))
                eng.wait_ge(a_v, t + 1)
                eng.wait_ge(a_pt, t + 1)
                eng.sem_inc(pe_begun, 1)
                ptv = pt[:, p, 0:512].rearrange("p (r g c) -> p r g c", r=4, g=2)
                for g in range(2):
                    for r in range(4):
                        for n in range(NPT):
                            last = eng.matmul(quad[32 * r:32 * r + 32, n, g * 64:g * 64 + 64],
                                              vs[32 * n:32 * n + 32, p, 32 * (4 * g + r):32 * (4 * g + r) + 32],
                                              ptv[32 * n:32 * n + 32, r, g, :], start=True, stop=True)
                last.then_inc(a_o_ps, 1)

            def project_a(t, p):
                eng.wait_ge(a_o, t + 1)
                need(eng, a_x1, t)
                if isinstance(t, int) and t == 0:
                    eng.wait_ge(wout_made, 2)
                for g in range(2):
                    for j in range(2):
                        last = eng.matmul(a_y, ot[:, p, 2 * g + j, :], wout[:, g, j, :],
                                          start=g + j == 0, stop=g + j == 2)
                last.then_inc(a_y_ps, 1)

            def step_a(i, p):
                if live(i):
                    scores_a(i, p)
                if live(i + 1):
                    transpose_x(i + 1, 1 - p, a_xh, a_xt, i + 1, a_t, a_xt_ps)
                if live(i - 1):
                    weigh_a(i - 1, 1 - p)
                if live(i + 1):
                    qkv(i + 1, 1 - p)
                if live(i - 1):
                    project_a(i - 1, 1 - p)

            eng.wait_ge(in_ident, 16)
            sweep(eng, step_a, 2)

            eng.wait_ge(in_cross_w, 16 * 14)
            for g in range(4):
                need(eng, products, 2 * g - 1)
                for h in range(4):
                    last = eng.matmul(bank[0][0:QC, h * KVC:(h + 1) * KVC], wuq_t[:, 4 * g + h, :], wuk_t[:, 4 * g + h, :],
                                      start=True, stop=True)
                last.then_inc(products_ps, 1)
                need(eng, products, 2 * g)
                for h in range(4):
                    c = 64 * (h % 2)
                    last = eng.matmul(bank[1][c:c + KVC, (h // 2) * E:(h // 2 + 1) * E], wuv_t[:, 4 * g + h, :], wo[:, 4 * g + h, :],
                                      start=True, stop=True)
                last.then_inc(products_ps, 1)
            for s, w in enumerate((wkr, wkr_s)):
                for k in range(KT):
                    last = eng.matmul(bank[2][:, (2 * s + k) * R:(2 * s + k + 1) * R], wkvc_t[:, k * P:(k + 1) * P], w[:, :],
                                      start=True, stop=True)
            last.then_inc(products_ps, 1)
            eng.wait_ge(ident_b_made, 1)
            eng.wait_ge(ternary_steps, 6)
            tern = quad[:, 0, 0:E].bitcast(BF16).rearrange("p (k n) -> p k n", k=KT)
            for k in range(KT):
                for n in range(KT):
                    last = eng.transpose(tern[:, k, n * P:(n + 1) * P], wff_q[:, n, k * P:(k + 1) * P], ident_b[:, :])
            last.then_inc(products_ps, 1)
            for n in range(KT):
                last = eng.matmul(quad[:, 1, n * P:(n + 1) * P], ones[:, :], gamma_d[:, n, :], start=True, stop=True)
            last.then_inc(products_ps, 1)

            def keys(t, p):
                eng.wait_ge(ctx_in[p], nth(t, p))
                need(eng, b_kr, t)
                need(eng, c_ffs, t - 3)
                for dst, w in ((b_knp, wkvc2), (b_krp[:, 0, :], wkr2), (b_krp[:, 1, :], wkr2_s)):
                    for k in range(KT):
                        last = eng.matmul(dst, w[:, k, :, :].rearrange("p d c -> p (d c)"), ctxt[:, p, k, :],
                                          start=k == 0, stop=k == KT - 1)
                last.then_inc(b_k_ps, 1)

            def key_rows(t, p):
                eng.wait_ge(b_kn, upto(t + 2))
                need(eng, c_ffs, t - 2)
                for k in range(KT):
                    last = eng.matmul(b_kvnp, ctxt[:, p, k, :], wkvc2[:, k, 0, :], start=k == 0, stop=k == KT - 1)
                last.then_inc(b_kvn_ps, 1)

            def q_c(t, p):
                eng.wait_ge(b_xt, t + 1)
                for k in range(KT):
                    last = eng.matmul(b_qcp, wdq[:, k, :], xt[:, p, k, :], start=k == 0, stop=k == KT - 1)
                last.then_inc(b_qc_ps, 1)

            def queries(t, p, part):
                eng.wait_ge(b_qc, t + 1)
                frees = ((b_rope, 4 * t - 1), (b_rope, 4 * t), (b_qn, 2 * t + 1), (b_qn, 2 * t + 2),
                         (b_rope, 4 * t + 1), (b_rope, 4 * t + 2))
                wn = wqn[:, :, :].rearrange("q h c -> q (h c)")
                turns = ((wn, 0), (wn, 4), (wqr, 0), (wqr_s, 0), (wqr, 4), (wqr_s, 4))
                for s in ((0, 1), (2, 3, 4, 5))[part]:
                    w, first = turns[s]
                    need(eng, *frees[s])
                    for h in range(4):
                        c = (first + h) * P
                        last = eng.matmul(bank[s % 2][:, h * P:(h + 1) * P], w[:, c:c + P], qct[:, p, :],
                                          start=True, stop=True)
                    last.then_inc(b_proj_ps, 1)

            def scores_b(t, p):
                eng.wait_ge(b_qn, 2 * t + 2)
                eng.wait_ge(b_qr, 2 * t + 2)
                eng.wait_ge(b_kn, t + 1)
                eng.wait_ge(b_kr, t + 1)
                need(eng, b_pt, 2 * (t - 1))
                eng.sem_inc(pe_begun, 1)
                for part, (q, k) in enumerate(((qn, kn), (qr, kr))):
                    for b in range(BPT):
                        for s in range(2):
                            rows = slice(64 * s, 64 * s + 64)
                            last = eng.matmul(quad[64 * b:64 * b + 64, s, :].rearrange("p (h q) -> p h q", h=HP),
                                              k[rows, p, 64 * b:64 * b + 64], q[rows, p, :, 64 * b:64 * b + 64],
                                              start=part == 0, stop=part == 1)
                last.then_inc(b_st_ps, 1)

            def turn_scores(t, p):
                eng.wait_ge(b_st, t + 1)
                need(eng, b_c, t - 1)
                for h in range(HP):
                    last = eng.transpose(quad[:, 2 + h // 4, h % 4 * P:(h % 4 + 1) * P], st[:, p, h * P:(h + 1) * P], ident[:, :])
                last.then_inc(b_s_ps, 1)

            def turn_p(t, p, s):
                eng.wait_ge(b_norm, t + 1)
                eng.wait_ge(b_st, upto(t + 2))
                for h in range(4):
                    last = eng.transpose(quad[:, s, h * P:(h + 1) * P], pn[:, p, (4 * s + h) * P:(4 * s + h + 1) * P],
                                         ident[:, :])
                last.then_inc(b_pt_ps, 1)

            def weigh_b(t, p):
                eng.wait_ge(b_kvn, t + 1)
                eng.wait_ge(b_pt, 2 * t + 2)
                eng.wait_ge(b_masked, upto(t + 2))
                eng.sem_inc(pe_begun, 1)
                pv = pt[:, p, :].rearrange("p (h s q) -> p h s q", h=HP, s=2)
                for s in range(2):
                    for b in range(BPT):
                        rows = slice(64 * b, 64 * b + 64)
                        last = eng.matmul(quad[64 * s:64 * s + 64, 2 + b, :].rearrange("p (h q) -> p h q", h=HP),
                                          kvn[rows, p, :], pv[rows, :, s, :], start=True, stop=True)
                last.then_inc(b_c_ps, 1)

            def project_b(t, p):
                eng.wait_ge(b_c, t + 1)
                eng.wait_ge(b_qc, upto(t + 3))
                for h in range(HP):
                    last = eng.matmul(b_y, ctxo[:, p, h, :], wvo[:, h, :], start=h == 0, stop=h == HP - 1)
                last.then_inc(b_y_ps, 1)

            def turn_quantised(t, p):
                eng.wait_ge(b_kr, upto(t + 4))
                eng.wait_ge(b_kvn, upto(t + 3))
                need(eng, c_ffs, t)
                eng.wait_ge(c_xq, t + 1)
                for k in range(KT):
                    last = eng.transpose(c_tp[:, k, :], xq[:, p, k * P:(k + 1) * P], ident_b[:, :])
                last.then_inc(c_t_ps, 1)

            def feed_forward(t, p):
                eng.wait_ge(c_t, t + 1)
                for k in range(KT):
                    last = eng.matmul(c_yp, xqt[:, p, k, :], wff_t[:, k, :], start=k == 0, stop=k == KT - 1)
                last.then_inc(c_y_ps, 1)

            def step_b(i, p):
                if live(i):
                    scores_b(i, p)
                if live(i + 1):
                    transpose_x(i + 1, 1 - p, b_xh, c_x2, i - 1, b_t, b_xt_ps)
                    keys(i + 1, 1 - p)
                if live(i):
                    key_rows(i, p)
                    turn_scores(i, p)
                if live(i - 1):
                    turn_p(i - 1, 1 - p, 0)
                    turn_p(i - 1, 1 - p, 1)
                if live(i + 1):
                    q_c(i + 1, 1 - p)
                    queries(i + 1, 1 - p, 0)
                if live(i - 1):
                    weigh_b(i - 1, 1 - p)
                if live(i + 1):
                    queries(i + 1, 1 - p, 1)
                if live(i - 2):
                    turn_quantised(i - 2, p)
                if live(i - 1):
                    project_b(i - 1, 1 - p)
                if live(i - 2):
                    feed_forward(i - 2, p)

            eng.wait_ge(products, 11)
            sweep(eng, step_b, 3)

        @block.vector
        def _(eng):
            def setup_a(i):
                if i == -2:
                    eng.wait_ge(in_window, 32)
                    eng.tensor_copy(seg_f[:, :, :], seg_i[:, :, :]).then_inc(seg_made, 1)
                    eng.wait_ge(in_masks, 32)
                if i == -1:
                    eng.wait_ge(in_wout, 16)
                    for j in range(2):
                        eng.tensor_scalar(wout[:, :, j, :], wout_n[:, :, :], parity[:, j:j + 1], None, ALU.mult).then_inc(wout_made, 1)
                if i == 1:
                    eng.wait_ge(in_ffn_w, 32)
                    eng.tensor_reduce(gamma[:, :], wff[:, :, :], AX.X, ALU.add, apply_absolute_value=True).then_inc(ternary_steps, 1)

            def statistics(t, p, src, arrived, count, stt, mvt, done, mean, normed):
                if arrived is not None:
                    eng.wait_ge(arrived, count)
                eng.bn_stats(stt[:, p, :], src).then_inc(done, 1)
                eng.wait_ge(done, t + 1)
                eng.sem_inc(dve_begun, 1)
                eng.bn_aggr(mvt[:, p, :], stt[:, p, :]).then_inc(mean, 1)

            def standardise(t, p, src, mvt, rt, dst, ready, used, used_at, done):
                eng.wait_ge(ready, t + 1)
                need(eng, used, used_at)
                eng.tensor_scalar(dst[:, p, :], src, mvt[:, p, 0:1], rt[:, p, :], ALU.subtract, ALU.mult).then_inc(done, 1)

            def mask_a(t, p):
                eng.wait_ge(a_s_ps, t + 1)
                need(eng, a_diff, t - 1)
                eng.tensor_tensor(sm[:, p, 0:512].rearrange("p (r g m) -> p r g m", r=4, g=4),
                                  quad[:, :, 0:P].rearrange("p r (g m) -> p r g m", g=4),
                                  causal[:, None, None, :].to_broadcast([P, 4, 4, L]), ALU.add).then_inc(a_masked, 1)

            def row_max(t, p, width, masked, done):
                eng.wait_ge(masked, t + 1)
                eng.tensor_reduce(mx[:, p, :], sm[:, p, 0:H * width].rearrange("p (h k) -> p h k", h=H),
                                  AX.X, ALU.max).then_inc(done, 1)

            def row_sum(t, p, width, exped, summed, done):
                eng.wait_ge(exped, t + 1)
                eng.tensor_reduce(rs[:, p, :], pe[:, p, 0:H * width].rearrange("p (h k) -> p h k", h=H),
                                  AX.X, ALU.add).then_inc(summed, 1)
                eng.wait_ge(summed, t + 1)
                eng.reciprocal(ri[:, p, :], rs[:, p, :]).then_inc(done, 1)

            def turn_p(t, p):
                eng.wait_ge(a_norm, t + 1)
                need(eng, a_o_ps, t - 1)
                eng.transpose(pt[:, p, 0:512], pn[:, p, 0:512]).then_inc(a_pt, 1)

            def residual_a(t, p):
                eng.wait_ge(a_y_ps, t + 1)
                if live(t - 2):
                    eng.wait_ge(x1_out[p], nth(t - 2, p))
                eng.tensor_tensor(x1[:, p, :], a_y, xall[:, t, :], ALU.add).then_inc(a_x1, 1)

            def step_a(i, p):
                if live(i):
                    mask_a(i, p)
                    row_max(i, p, L, a_masked, a_max)
                if live(i + 2):
                    statistics(i + 2, p, xall[:, i + 2, :], x_in[p], nth(i + 2, p), stat, mv, a_stat, a_mean, a_xh)
                if live(i):
                    row_sum(i, p, L, a_exp, a_sum, a_rec)
                if live(i + 2):
                    standardise(i + 2, p, xall[:, i + 2, :], mv, rstd, xh, a_rstd, a_xt_ps, i + 1, a_xh)
                if live(i):
                    turn_p(i, p)
                if live(i - 1):
                    residual_a(i - 1, 1 - p)
                if isinstance(i, int):
                    setup_a(i)

            eng.wait_ge(fills, 3)
            sweep(eng, step_a, 2)

            eng.wait_ge(ternary_steps, 1)
            eng.tensor_scalar(gamma_e[:, :], gamma[:, :], 1.0 / E, Q_EPS, ALU.mult, ALU.add).then_inc(ternary_steps, 1)
            eng.wait_ge(ternary_steps, 2)
            eng.reciprocal(gamma_r[:, :], gamma_e[:, :]).then_inc(ternary_steps, 1)
            eng.wait_ge(ternary_steps, 3)
            for k in range(KT):
                eng.tensor_scalar(wff_n[:, k, :], wff[:, k, :], gamma_r[:, k:k + 1], ROUND, ALU.mult, ALU.add)
                last = eng.tensor_scalar(gamma_d[:, k, :], ident[:, :], gamma[:, k:k + 1], 1.0 / E, ALU.mult, ALU.mult)
            last.then_inc(ternary_steps, 1)
            eng.wait_ge(ternary_steps, 4)
            eng.tensor_scalar(wff[:, :, :], wff_n[:, :, :], ROUND + 1.0, ROUND - 1.0, ALU.min, ALU.max).then_inc(ternary_steps, 1)
            eng.wait_ge(ternary_steps, 5)
            eng.tensor_scalar(wff_q[:, :, :], wff[:, :, :], -ROUND, None, ALU.add).then_inc(ternary_steps, 1)

            def mask_b(t, p):
                eng.wait_ge(b_s_ps, t + 1)
                need(eng, b_diff, t - 1)
                eng.tensor_tensor(sm[:, p, :].rearrange("p (h k) -> p h k", h=HP),
                                  quad[:, 2:4, :].rearrange("p s (h k) -> p (s h) k", h=4),
                                  window[:, t, None, :].to_broadcast([P, HP, P]), ALU.add).then_inc(b_masked, 1)

            def rope_keys(t, p):
                eng.wait_ge(b_kn, t + 1)
                need(eng, b_kvn, t)
                for dst, s, table in ((kr_a, 0, cos_t), (kr_b, 1, sin_t)):
                    last = eng.tensor_tensor(dst[:, :].rearrange("p (b k) -> p b k", b=BPT),
                                             b_krp[:, s, :].rearrange("p (b k) -> p b k", b=BPT),
                                             table[:, None, :].to_broadcast([P, BPT, N]), ALU.mult)
                last.then_inc(b_kr_ab, 1)
                eng.wait_ge(b_kr_ab, t + 1)
                need(eng, b_st_ps, t - 1)
                eng.tensor_tensor(kr[:, p, :], kr_a[:, :], kr_b[:, :], ALU.add).then_inc(b_kr, 1)

            def rope_queries(t, p, s):
                for part, (dst, table) in enumerate(((qr_a, cos_t), (qr_b, sin_t))):
                    eng.wait_ge(b_proj_ps, 6 * t + 2 * s + part + 3)
                    need(eng, b_qr, 2 * t + s - 1)
                    eng.tensor_tensor(dst[:, s, :].rearrange("p (h q) -> p h q", q=N),
                                      bank[part][:, :].rearrange("p (h q) -> p h q", q=N),
                                      table[:, None, :].to_broadcast([P, HP, N]), ALU.mult).then_inc(b_rope, 1)

            def residual_b(t, p):
                eng.wait_ge(b_y_ps, t + 1)
                need(eng, c_x2b, t - 1)
                eng.tensor_tensor(x2[:, p, :], b_y, xall[:, t, :], ALU.add).then_inc(c_x2, 1)

            def largest(t, p):
                eng.wait_ge(c_h, t + 1)
                eng.tensor_reduce(mh[:, p, :], h3[:, p, :], AX.X, ALU.max, apply_absolute_value=True).then_inc(c_mh, 1)

            def quantise(t, p):
                eng.wait_ge(c_rq, t + 1)
                eng.wait_ge(c_mh, t + 1)
                steps = 6 * t
                eng.tensor_scalar(xs[:, p, :], mh[:, p, :], rq[:, p, :], 1.0 / QB, ALU.mult, ALU.mult).then_inc(c_scale, 1)
                eng.wait_ge(c_scale, steps + 1)
                eng.tensor_scalar(xse[:, p, :], xs[:, p, :], Q_EPS, None, ALU.add).then_inc(c_scale, 1)
                eng.wait_ge(c_scale, steps + 2)
                eng.reciprocal(xsr[:, p, :], xse[:, p, :]).then_inc(c_scale, 1)
                eng.wait_ge(c_scale, steps + 3)
                eng.tensor_scalar(hc[:, p, :], h3[:, p, :], rq[:, p, :], None, ALU.mult).then_inc(c_scale, 1)
                eng.wait_ge(c_scale, steps + 4)
                eng.tensor_scalar(hr[:, p, :], hc[:, p, :], xsr[:, p, :], ROUND, ALU.mult, ALU.add).then_inc(c_scale, 1)
                eng.wait_ge(c_scale, steps + 5)
                eng.tensor_scalar(hc[:, p, :], hr[:, p, :], ROUND + QB, ROUND - QB, ALU.min, ALU.max).then_inc(c_scale, 1)
                eng.wait_ge(c_scale, steps + 6)
                need(eng, c_t_ps, t - 1)
                eng.tensor_scalar(xq[:, p, :], hc[:, p, :], -ROUND, None, ALU.add).then_inc(c_xq, 1)

            def finish(t, p):
                eng.wait_ge(c_y_ps, t + 1)
                eng.scalar_tensor_tensor(ffs[:, p, :], c_yp, xs[:, p, :], gamma_b[:, :], ALU.mult, ALU.mult).then_inc(c_ffs, 1)
                eng.wait_ge(c_ffs, t + 1)
                eng.wait_ge(c_x2b, t + 1)
                if live(t - 2):
                    eng.wait_ge(out_done[p], nth(t - 2, p))
                eng.tensor_tensor(res[:, p, :], ffs[:, p, :], x2b[:, p, :], ALU.add).then_inc(c_out, 1)

            def step_b(i, p):
                if live(i - 3):
                    finish(i - 3, 1 - p)
                if live(i - 2):
                    residual_b(i - 2, p)
                    statistics(i - 2, p, x2[:, p, :], c_x2, i - 1, stat3, mv3, c_stat, c_mean, c_h)
                    standardise(i - 2, p, x2[:, p, :], mv3, rstd3, h3, c_rstd, c_ssq, i - 3, c_h)
                    largest(i - 2, p)
                if live(i):
                    mask_b(i, p)
                    row_max(i, p, N, b_masked, b_max)
                if live(i + 2):
                    statistics(i + 2, p, xall[:, i + 2, :], x1_in[p], nth(i + 2, p), stat, mv, b_stat, b_mean, b_xh)
                if live(i + 1):
                    rope_keys(i + 1, 1 - p)
                if live(i - 2):
                    quantise(i - 2, p)
                if live(i + 2):
                    standardise(i + 2, p, xall[:, i + 2, :], mv, rstd, xh, b_rstd, b_xt_ps, i + 1, b_xh)
                if live(i + 1):
                    rope_queries(i + 1, 1 - p, 0)
                    rope_queries(i + 1, 1 - p, 1)
                if live(i):
                    row_sum(i, p, N, b_exp, b_sum, b_rec)

            eng.wait_ge(products, 11)
            eng.wait_ge(window_steps, 4)
            sweep(eng, step_b, 3)


def swap_halves(w, heads):
    k = w.shape[0]
    return np.ascontiguousarray(w.reshape(k, heads, 2, R // 2)[:, :, ::-1, :].reshape(k, heads * R))


def shape_constants():
    half = R // 2
    inv_freq = (np.float32(1.0) / np.power(np.float32(10000.0), np.arange(half, dtype=np.float32) / np.float32(half))).astype(np.float32)
    ang = (np.arange(N, dtype=np.float32)[:, None] * inv_freq).astype(np.float32)
    cos, sin = np.cos(ang).T, np.sin(ang).T
    row = np.arange(P)
    return {
        "ident_c": np.eye(P, dtype=np.float32),
        "causal_c": np.where(np.arange(L)[None, :] <= (row % L)[:, None], 0.0, NEG).astype(np.float32),
        "parity_c": ((row // DH % 2)[:, None] == np.arange(2)[None, :]).astype(np.float32),
        "cos_c": np.concatenate([cos, cos, cos, cos]).astype(np.float32),
        "sin_c": np.concatenate([-sin, sin, -sin, sin]).astype(np.float32),
        "kidx_c": np.tile(np.arange(N, dtype=np.float32), (P, 1)),
    }


def kernel(x, ctx_2048, itok_BxS_0_1023, L0_attn_weight_qkv, L0_attn_weight_out, L0_xattn_W_kvc, L0_xattn_W_dq,
           L0_xattn_W_uq, L0_xattn_W_qr, L0_xattn_W_uk, L0_xattn_W_kr, L0_xattn_W_uv, L0_xattn_W_o,
           L0_ffn_weight, L0_ffn_bias):
    import concourse.bacc as _bacc
    from concourse.bass_utils import run_bass_kernel_spmd as _run

    lay = np.ascontiguousarray
    a = {
        "x": lay(x),
        "ctx_t": lay(np.asarray(ctx_2048).reshape(NT, P, KT, P).transpose(0, 3, 2, 1).reshape(NT, P, KT * P)),
        "seg": lay(np.tile(np.asarray(itok_BxS_0_1023).reshape(NT, BPT, N).transpose(2, 0, 1), (2, 1, 1))),
        "w_qkv_t": lay(np.asarray(L0_attn_weight_qkv).T),
        "w_out_t": lay(np.asarray(L0_attn_weight_out).T),
        "w_kvc": lay(L0_xattn_W_kvc),
        "w_kvc_t": lay(np.asarray(L0_xattn_W_kvc).T),
        "w_dq": lay(L0_xattn_W_dq),
        "w_uq_t": lay(np.asarray(L0_xattn_W_uq).reshape(QC, H, HD).transpose(2, 1, 0)),
        "w_qr": lay(L0_xattn_W_qr),
        "w_qr_s": swap_halves(np.asarray(L0_xattn_W_qr), H),
        "w_uk_t": lay(np.asarray(L0_xattn_W_uk).reshape(KVC, H, HD).transpose(2, 1, 0)),
        "w_kr": lay(L0_xattn_W_kr),
        "w_kr_s": swap_halves(np.asarray(L0_xattn_W_kr), 1),
        "w_uv_t": lay(np.asarray(L0_xattn_W_uv).reshape(KVC, H, HD).transpose(2, 1, 0)),
        "w_o": lay(np.asarray(L0_xattn_W_o).reshape(H, HD, E).transpose(1, 0, 2)),
        "w_ff": lay(L0_ffn_weight),
        "b_ff": lay(np.asarray(L0_ffn_bias).reshape(1, E)),
    }
    a.update(shape_constants())
    nc = _bacc.Bacc("TRN2", target_bir_lowering=False, num_devices=1)
    args = {n: nc.dram_tensor(n, v.shape, mybir.dt.from_np(v.dtype), kind="ExternalInput").ap() for n, v in a.items()}
    x1_dram = nc.dram_tensor("x1_dram", (L, N, E), F32, kind="Internal").ap()
    out = nc.dram_tensor("out", (L, N, E), F32, kind="ExternalOutput").ap()
    decoder_layer(nc, x1_dram=x1_dram, out=out, **args)
    return _run(nc, [a], core_ids=[0]).results[0]["out"]
```

```python
from contextlib import ExitStack

import numpy as np

import concourse.bass as bass
from concourse import mybir

P = 128
E = 256
KT = E // P
NT = 16
L, N = 32, 64
H = 16
DH = 16
NPT = P // L
BPT = P // N
HP = H // 2
KVC, QC, R, HD = 64, 96, 64, 128
LOOKBACK = 8
NEG = -1e30
LN_EPS = 1e-5
Q_EPS = 1e-8
QB = 127.0
ROUND = 12582912.0
SELF_SCALE = DH ** -0.5
CROSS_SCALE = float(np.float32(1.0) / np.sqrt(HD + R).astype(np.float32))

ALU = mybir.AluOpType
ACT = mybir.ActivationFunctionType
AX = mybir.AxisListType
F32 = mybir.dt.float32
BF16 = mybir.dt.bfloat16
I32 = mybir.dt.int32


def need(eng, sem, count):
    if not isinstance(count, int) or count > 0:
        eng.wait_ge(sem, count)


def live(t):
    return not isinstance(t, int) or 0 <= t < NT


def self_finished(i, p):
    if not isinstance(i, int) or i < NT:
        return [(i - 3, 1 - p)] if live(i - 3) else []
    return {NT: [(NT - 3, 1 - p), (NT - 2, p)], NT + 1: [(NT - 1, p)]}.get(i, [])


def softmax_on_vector(i):
    return isinstance(i, int) and i == NT - 1


def upto(t):
    return min(t, NT) if isinstance(t, int) else t


def nth(t, p):
    return 8 * (t - p + 2)


def sweep(eng, step, first):
    for i in range(-2, 2 * first):
        step(i, i % 2)
    with eng.Fori(first, NT // 2 - 1) as j:
        for p in range(2):
            step(2 * j + p, p)
    for i in range(NT - 2, NT + 4):
        step(i, i % 2)


def decoder_layer(nc, x, ctx_t, seg, w_qkv_t, w_out_t, w_kvc, w_kvc_t, w_dq, w_uq_t, w_qr,
                  w_uk_t, w_kr, w_uv_t, w_o, w_ff, b_ff, ident_c, causal_c, parity_c,
                  cos_c, sin_c, kidx_c, x1_dram, out):
    with ExitStack() as ctx:
        def sb(name, shape, dt=F32):
            return ctx.enter_context(nc.sbuf_tensor(name, shape, dt))

        def sem(name):
            return ctx.enter_context(nc.semaphore(name))

        bank = [ctx.enter_context(nc.psum_tensor(f"bank{i}", [P, 512], F32)) for i in range(4)]
        quad = ctx.enter_context(nc.psum_tensor("quad", [P, 4, 512], F32))

        ident = sb("ident", [P, P])
        ident_b = sb("ident_b", [P, P], BF16)
        ones = sb("ones", [P, P])
        neg_half = sb("neg_half", [P, 1])
        table_loaded = sb("table_loaded", [P, 1])
        ln_eps = sb("ln_eps", [P, 1])
        causal = sb("causal", [P, L])
        parity = sb("parity", [P, 2])
        cos_t = sb("cos_t", [P, N])
        sin_t = sb("sin_t", [P, N])
        kidx = sb("kidx", [P, N])
        seg_i = sb("seg_i", [P, NT, BPT], I32)
        seg_f = sb("seg_f", [P, NT, BPT])
        window = sb("window", [P, NT, P])
        window4 = window[:, :, :].rearrange("p t (b k) -> p t b k", b=BPT)
        wqkv = sb("wqkv", [P, KT, 3 * E])
        wout = sb("wout", [P, KT, E])
        wk = sb("wk", [P, KT, KVC + R])
        wkvc_t = sb("wkvc_t", [KVC, E])
        wdq = sb("wdq", [P, KT, QC])
        wuq_t = sb("wuq_t", [P, H, QC])
        st = sb("st", [P, 2, 1024])
        wuk_t = st[:, 0, :].rearrange("p (h c) -> p h c", h=H)
        wuv_t = st[:, 1, :].rearrange("p (h c) -> p h c", h=H)
        wkr = sb("wkr", [KVC, R])
        qall = sb("qall", [P, 2, H, P])
        wo = qall[:, :, :, :].rearrange("p a h t -> p (a h t)").rearrange("p (h e) -> p h e", h=H)
        wq_latent = sb("wq_latent", [QC, HP, 2 * KVC])
        wq_rope = sb("wq_rope", [QC, HP, 2 * R])
        wvo = sb("wvo", [P, HP, E])
        wff = sb("wff", [P, KT, E])
        wff_n = sb("wff_n", [P, KT, E])
        wff_q = sb("wff_q", [P, KT, E], BF16)
        wff_t = sb("wff_t", [P, KT, E], BF16)
        gamma = sb("gamma", [P, KT])
        gamma_e = sb("gamma_e", [P, KT])
        gamma_r = sb("gamma_r", [P, KT])
        gamma_d = sb("gamma_d", [P, KT, P])
        gamma_b = sb("gamma_b", [P, E])
        bias_b = sb("bias_b", [P, E])

        xall = sb("xall", [P, NT, E])
        stat = sb("stat", [P, 2, 6])
        mv = sb("mv", [P, 2, 2])
        ve = sb("ve", [P, 2, 1])
        rstd = sb("rstd", [P, 2, 1])
        xh = sb("xh", [P, 2, E])
        xt = sb("xt", [P, 2, KT, P])
        qt = sb("qt", [P, 2, 2, P])
        kx = sb("kx", [P, 2, 2, 2, P])
        vs = sb("vs", [P, 2, E])
        sm = sb("sm", [P, 2, 1024])
        sd = sb("sd", [P, 2, 1024])
        pe = sb("pe", [P, 2, 1024])
        pn = sb("pn", [P, 2, 1024])
        mx = sb("mx", [P, 2, H])
        rs = sb("rs", [P, 2, H])
        ri = sb("ri", [P, 2, H])
        pt = sb("pt", [P, 2, 1024])
        ot_even = sb("ot_even", [P, 2, E])
        ot = sb("ot", [P, 2, KT, P])
        x1 = sb("x1", [P, 2, E])
        ctxt = sb("ctxt", [P, 2, KT, P])
        kall = sb("kall", [P, 2, 2, P])
        k_sw = sb("k_sw", [P, P])
        q_rope = sb("q_rope", [P, HP, P])
        q_sw = sb("q_sw", [P, HP, P])
        kvn = sb("kvn", [P, 2, KVC])
        qct = sb("qct", [QC, 2, P])
        ctxo = sb("ctxo", [P, 2, HP, P])
        window2 = ctxo[:, :, :, :].rearrange("p a h t -> p (a h) t")
        x2 = sb("x2", [P, 2, E])
        x2b = sb("x2b", [P, 2, E])
        stat3 = sb("stat3", [P, 2, 6])
        mv3 = sb("mv3", [P, 2, 2])
        ve3 = sb("ve3", [P, 2, 1])
        rstd3 = sb("rstd3", [P, 2, 1])
        h3 = sb("h3", [P, 2, E])
        hsq = sb("hsq", [P, 2, E])
        ssq = sb("ssq", [P, 2, 1])
        mh = sb("mh", [P, 2, 1])
        vq = sb("vq", [P, 2, 1])
        rq = sb("rq", [P, 2, 1])
        xs = sb("xs", [P, 2, 1])
        xse = sb("xse", [P, 2, 1])
        xsr = sb("xsr", [P, 2, 1])
        fq = sb("fq", [P, 2, 1])
        hr = sb("hr", [P, 2, E])
        hc = sb("hc", [P, 2, E])
        xq = sb("xq", [P, 2, E], BF16)
        xqt = sb("xqt", [P, 2, KT, P], BF16)
        ffs = sb("ffs", [P, 2, E])
        res = sb("res", [P, 2, E])

        in_ident, in_wqkv, in_masks, in_wout, in_window, in_cross_w, in_ffn_w = (sem(s) for s in (
            "in_ident", "in_wqkv", "in_masks", "in_wout", "in_window", "in_cross_w", "in_ffn_w"))
        fills = sem("fills")
        pe_begun, dve_begun = sem("pe_begun"), sem("dve_begun")
        ident_b_made, seg_made, window_steps, ternary_steps, products_ps, products = (sem(s) for s in (
            "ident_b_made", "seg_made", "window_steps", "ternary_steps", "products_ps", "products"))
        x_in = [sem(f"x_in{p}") for p in range(2)]
        x1_out = [sem(f"x1_out{p}") for p in range(2)]
        x1_in = [sem(f"x1_in{p}") for p in range(2)]
        ctx_in = [sem(f"ctx_in{p}") for p in range(2)]
        out_done = [sem(f"out_done{p}") for p in range(2)]
        a_stat, a_mean, a_var, a_rstd, a_xh = (sem(s) for s in ("a_stat", "a_mean", "a_var", "a_rstd", "a_xh"))
        a_xt_ps, a_xt, a_q_ps, a_q, a_k_ps, a_k, a_v_ps, a_v = (sem(s) for s in (
            "a_xt_ps", "a_xt", "a_q_ps", "a_q", "a_k_ps", "a_k", "a_v_ps", "a_v"))
        a_s_ps, a_masked, a_max, a_diff, a_exp, a_sum, a_rec, a_norm, a_pt = (sem(s) for s in (
            "a_s_ps", "a_masked", "a_max", "a_diff", "a_exp", "a_sum", "a_rec", "a_norm", "a_pt"))
        a_o_ps, a_o_even, a_o, a_y_ps, a_x1 = (sem(s) for s in ("a_o_ps", "a_o_even", "a_o", "a_y_ps", "a_x1"))
        b_stat, b_mean, b_var, b_rstd, b_xh = (sem(s) for s in ("b_stat", "b_mean", "b_var", "b_rstd", "b_xh"))
        b_xt_ps, b_xt, b_qc_ps, b_qc = (sem(s) for s in ("b_xt_ps", "b_xt", "b_qc_ps", "b_qc"))
        b_k_ps, b_k_out, b_k_parts, b_k, b_k_turned, b_kvn_ps, b_kvn = (sem(s) for s in (
            "b_k_ps", "b_k_out", "b_k_parts", "b_k", "b_k_turned", "b_kvn_ps", "b_kvn"))
        b_q_ps, b_q_out, b_q_parts, b_q_first, b_q_second = (sem(s) for s in (
            "b_q_ps", "b_q_out", "b_q_parts", "b_q_first", "b_q_second"))
        q_swapped = sem("q_swapped")
        b_st_ps, b_st, b_s_ps, b_masked, b_max, b_diff, b_exp, b_sum, b_rec, b_norm = (sem(s) for s in (
            "b_st_ps", "b_st", "b_s_ps", "b_masked", "b_max", "b_diff", "b_exp", "b_sum", "b_rec", "b_norm"))
        b_pt_ps, b_pt, b_c_ps, b_c, b_y_ps = (sem(s) for s in ("b_pt_ps", "b_pt", "b_c_ps", "b_c", "b_y_ps"))
        c_x2, c_x2b, c_stat, c_mean, c_var, c_rstd, c_h, c_ssq, c_mh = (sem(s) for s in (
            "c_x2", "c_x2b", "c_stat", "c_mean", "c_var", "c_rstd", "c_h", "c_ssq", "c_mh"))
        c_vq, c_rq, c_scale, c_xq = (sem(s) for s in ("c_vq", "c_rq", "c_scale", "c_xq"))
        c_t_ps, c_t, c_y_ps, c_ffs, c_out = (sem(s) for s in ("c_t_ps", "c_t", "c_y_ps", "c_ffs", "c_out"))

        x_cols = x.rearrange("l (t n) e -> t n l e", n=NPT)
        x1_cols = x1_dram.rearrange("l (t n) e -> t n l e", n=NPT)
        x1_rows = x1_dram.rearrange("(t b) n e -> t (b n) e", b=BPT)
        out_rows = out.rearrange("(t b) n e -> t (b n) e", b=BPT)

        a_t = bank[0][:, 0:E].rearrange("p (k t) -> p k t", k=KT)
        a_qp = bank[1][:, 0:E].rearrange("p (f t) -> p f t", f=KT)
        a_vp = bank[0][:, E:2 * E]
        a_kp = bank[2][:, 0:E].rearrange("p (f t) -> p f t", f=KT)
        a_y = bank[3][:, 0:E]
        heads = quad[:, :, 0:P].rearrange("p n (g j l) -> p n g j l", g=KT, j=2)
        b_t = bank[2][:, 0:E].rearrange("p (k t) -> p k t", k=KT)
        b_qcp = bank[2][0:QC, E:E + P]
        b_y = bank[2][:, 0:E]
        b_kp = bank[3][:, 0:P]
        b_kvnp = bank[3][:, P:P + KVC]
        c_tp = bank[3][:, 0:P].bitcast(BF16).rearrange("p (k t) -> p k t", k=KT)
        c_yp = bank[3][:, 0:E]

        quarter = [slice(R // 2 * q, R // 2 * (q + 1)) for q in range(4)]
        halves = [(quarter[q], quarter[q ^ 1]) for q in range(4)]
        rows = (slice(0, 64), slice(64, P))

        q_heads = [qall[:, p, :, :].rearrange("c (h s) t -> c s h t", s=2) for p in range(2)]

        def add_rope(eng, p, g, done):
            for s in range(2):
                own = rows[1 - s]
                eng.tensor_tensor(q_heads[p][own, s, 4 * g:4 * g + 4, :], q_rope[own, 4 * g:4 * g + 4, :],
                                  q_sw[own, 4 * g:4 * g + 4, :], ALU.add).then_inc(done, 1)

        def submax(eng, t, p, width, maxed, exped, done):
            eng.wait_ge(maxed, t + 1)
            need(eng, exped, t - 1)
            m = H * width
            eng.tensor_tensor(sd[:, p, 0:m].rearrange("p (h k) -> p h k", h=H),
                              sm[:, p, 0:m].rearrange("p (h k) -> p h k", h=H),
                              mx[:, p, :, None].to_broadcast([P, H, width]), ALU.subtract).then_inc(done, 1)

        def normalise(eng, t, p, width, recip, used, uses, done):
            eng.wait_ge(recip, t + 1)
            need(eng, used, uses * (t - 1))
            m = H * width
            eng.tensor_tensor(pn[:, p, 0:m].rearrange("p (h k) -> p h k", h=H),
                              pe[:, p, 0:m].rearrange("p (h k) -> p h k", h=H),
                              ri[:, p, :, None].to_broadcast([P, H, width]), ALU.mult).then_inc(done, 1)

        product_kinds = [("ternary", 0), ("gamma", 0), ("keys", 0)] + [("queries", g) for g in range(4)] + [("values", g) for g in range(4)]
        product_turns = {NT - 1: range(0, 3), NT: (3,), NT + 3: range(4, 11)}

        block = ctx.enter_context(nc.Block())

        @block.sync
        def _(eng):
            def load_x(t, p):
                need(eng, a_stat, t - 1)
                eng.dma_start(xall[:, t, :], x_cols[t]).then_inc(x_in[p], 16)

            load_x(0, 0)
            load_x(1, 1)
            eng.dma_start(parity[:, :], parity_c).then_inc(in_masks, 16)
            eng.dma_start(causal[:, :], causal_c).then_inc(in_masks, 16)
            eng.dma_start(wout[:, :, :], w_out_t.rearrange("(k p) f -> p k f", p=P)).then_inc(in_wout, 16)
            eng.dma_start(seg_i[:, :, :], seg).then_inc(in_window, 16)
            eng.dma_start(kidx[:, :], kidx_c).then_inc(in_window, 16)
            eng.dma_start(wff[:, :, :], w_ff.rearrange("(k p) f -> p k f", p=P)).then_inc(in_ffn_w, 16)
            eng.dma_start(bias_b[:, :], b_ff.to_broadcast([P, E])).then_inc(in_ffn_w, 16)

            def load_cross_weights():
                eng.dma_start(cos_t[:, :], cos_c).then_inc(in_cross_w, 16)
                eng.dma_start(sin_t[:, :], sin_c).then_inc(in_cross_w, 16)
                eng.dma_start(wk[:, :, 0:KVC], w_kvc.rearrange("(k p) c -> p k c", p=P)).then_inc(in_cross_w, 16)
                w_qr_pairs = w_qr.rearrange("q (h s r) -> s q h r", h=HP, s=2)
                for s in range(2):
                    eng.dma_start(wq_rope[:, :, R * (1 - s):R * (2 - s)], w_qr_pairs[s]).then_inc(in_cross_w, 16)
                for dst, src in ((wkvc_t, w_kvc_t), (wkr, w_kr)):
                    eng.dma_start(dst[:, :], src).then_inc(in_cross_w, 16)
                eng.dma_start(wdq[:, :, :], w_dq.rearrange("(k p) c -> p k c", p=P)).then_inc(in_cross_w, 16)
                for dst, src in ((wuq_t[:, :, :], w_uq_t), (wuk_t, w_uk_t), (wuv_t, w_uv_t), (wo, w_o)):
                    eng.dma_start(dst, src).then_inc(in_cross_w, 16)

            def store_x1(t, p):
                eng.wait_ge(a_x1, t + 1)
                eng.dma_start(x1_cols[t], x1[:, p, :]).then_inc(x1_out[p], 16)

            def step_a(i, p):
                if live(i + 2) and not (isinstance(i, int) and i < 0):
                    load_x(i + 2, p)
                if isinstance(i, int) and i == 1:
                    load_cross_weights()
                for t, parity_t in self_finished(i, p):
                    store_x1(t, parity_t)

            sweep(eng, step_a, 2)

            for p in range(2):
                eng.wait_ge(x1_out[p], 16 * NT // 2)

            def load_b(t, p):
                need(eng, b_stat, t - 1)
                eng.dma_start(xall[:, t, :], x1_rows[t]).then_inc(x1_in[p], 16)
                need(eng, b_kvn_ps, t - 1)
                eng.dma_start(ctxt[:, p, :, :], ctx_t[t].rearrange("p (k t) -> p k t", k=KT)).then_inc(ctx_in[p], 16)

            def store_out(t, p):
                eng.wait_ge(c_out, t + 1)
                eng.dma_start(out_rows[t], res[:, p, :]).then_inc(out_done[p], 16)

            def swap_halves(t):
                eng.wait_ge(b_q_out, 4 * t + 2)
                for to, half in halves:
                    eng.dma_start(q_sw[to, :, :], q_rope[half, :, :]).then_inc(q_swapped, 16)

            def step_b(i, p):
                if live(i + 2):
                    load_b(i + 2, p)
                if live(i + 1):
                    swap_halves(i + 1)
                if live(i - 3):
                    store_out(i - 3, 1 - p)

            sweep(eng, step_b, 3)
            for p in range(2):
                eng.wait_ge(out_done[p], 16 * NT // 2)

        @block.gpsimd
        def _(eng):
            eng.memset(ones[:, :], 1.0).then_inc(fills, 1)
            eng.memset(neg_half[:, :], -0.5).then_inc(fills, 1)
            eng.memset(ln_eps[:, :], LN_EPS).then_inc(fills, 1)
            eng.wait_ge(fills, 3)
            def inverse_root(t, p, mean, mvt, vet, var, rt, done):
                eng.wait_ge(mean, t + 1)
                eng.tensor_tensor(vet[:, p, :], mvt[:, p, 1:2], ln_eps[:, :], ALU.add).then_inc(var, 1)
                eng.wait_ge(var, t + 1)
                eng.tensor_tensor(rt[:, p, :], vet[:, p, :], neg_half[:, :], ALU.pow).then_inc(done, 1)

            def step_a(i, p):
                if live(i):
                    submax(eng, i, p, L, a_max, a_exp, a_diff)
                if live(i + 2):
                    inverse_root(i + 2, p, a_mean, mv, ve, a_var, rstd, a_rstd)
                if live(i):
                    normalise(eng, i, p, L, a_rec, a_pt, 1, a_norm)
                if isinstance(i, int) and i == NT:
                    eng.wait_ge(seg_made, 1)
                    eng.tensor_tensor(window4, kidx[:, None, None, :].to_broadcast([P, NT, BPT, N]),
                                      seg_f[:, :, :, None].to_broadcast([P, NT, BPT, N]), ALU.subtract).then_inc(window_steps, 1)

            sweep(eng, step_a, 2)

            def biased(t, p):
                eng.wait_ge(c_x2, t + 1)
                need(eng, c_out, t - 1)
                eng.tensor_tensor(x2b[:, p, :], x2[:, p, :], bias_b[:, :], ALU.add).then_inc(c_x2b, 1)

            def add_feed_forward(t, p):
                eng.wait_ge(c_ffs, t + 1)
                eng.wait_ge(c_x2b, t + 1)
                if live(t - 2):
                    eng.wait_ge(out_done[p], nth(t - 2, p))
                eng.tensor_tensor(res[:, p, :], ffs[:, p, :], x2b[:, p, :], ALU.add).then_inc(c_out, 1)

            def inverse_rms(t, p):
                need(eng, c_xq, t - 1)
                eng.wait_ge(c_vq, t + 1)
                eng.tensor_tensor(rq[:, p, :], vq[:, p, :], neg_half[:, :], ALU.pow).then_inc(c_rq, 1)

            def step_b(i, p):
                if live(i - 2):
                    inverse_root(i - 2, p, c_mean, mv3, ve3, c_var, rstd3, c_rstd)
                if live(i + 2):
                    inverse_root(i + 2, p, b_mean, mv, ve, b_var, rstd, b_rstd)
                if live(i - 2):
                    inverse_rms(i - 2, p)
                    biased(i - 2, p)
                if live(i - 3):
                    add_feed_forward(i - 3, 1 - p)
                if live(i) and not softmax_on_vector(i):
                    submax(eng, i, p, N, b_max, b_exp, b_diff)
                if live(i + 1):
                    eng.wait_ge(b_rstd, upto(i + 3))
                    need(eng, c_x2b, i - 1)
                    need(eng, c_out, i - 2)
                    if live(i):
                        eng.wait_ge(b_diff, i + 1)
                    eng.wait_ge(b_q_parts, 2 * (i + 1) + 1)
                    add_rope(eng, 1 - p, 1, b_q_second)
                    eng.wait_ge(b_q_second, 2 * (i + 1) + 2)
                if live(i) and not softmax_on_vector(i):
                    normalise(eng, i, p, N, b_rec, b_pt_ps, 2, b_norm)

            eng.wait_ge(in_ffn_w, 32)
            sweep(eng, step_b, 3)

        @block.scalar
        def _(eng):
            eng.dma_start(ident[:, :], ident_c).then_inc(in_ident, 16)
            for k in range(KT):
                eng.dma_start(wqkv[:, k, :], w_qkv_t[k * P:(k + 1) * P, :]).then_inc(in_wqkv, 16)
            eng.wait_ge(fills, 1)
            eng.activation(table_loaded[:, :], ones[:, 0:1], ACT.Exp)

            def x_t(t, p, made, used, done, src):
                eng.wait_ge(made, t + 1)
                need(eng, used, t - 1)
                eng.activation(xt[:, p, :, :], src, ACT.Copy).then_inc(done, 1)

            def even_heads_out(t, p):
                eng.wait_ge(a_o_ps, t + 1)
                need(eng, a_o, t - 1)
                eng.activation(ot_even[:, p, :].rearrange("p (g n l) -> p n g l", g=KT, n=NPT), heads[:, :, :, 0, :], ACT.Copy,
                               scale=parity[:, 0:1]).then_inc(a_o_even, 1)

            def exps(t, p, width, scale, diff, normed, done):
                eng.wait_ge(diff, t + 1)
                need(eng, normed, t - 1)
                eng.activation(pe[:, p, 0:H * width], sd[:, p, 0:H * width], ACT.Exp, scale=scale).then_inc(done, 1)

            def queries(t, p):
                eng.wait_ge(a_q_ps, t + 1)
                need(eng, a_s_ps, t - 1)
                eng.activation(qt[:, p, :, :], a_qp, ACT.Copy).then_inc(a_q, 1)

            def values(t, p):
                eng.wait_ge(a_v_ps, t + 1)
                need(eng, a_o_ps, t - 1)
                eng.activation(vs[:, p, :], a_vp, ACT.Copy).then_inc(a_v, 1)

            def keys(t, p):
                eng.wait_ge(a_k_ps, t + 1)
                need(eng, a_s_ps, t - 1)
                if isinstance(t, int) and t == 0:
                    eng.wait_ge(in_masks, 32)
                for j in range(2):
                    last = eng.activation(kx[:, p, :, j, :], a_kp, ACT.Copy, scale=parity[:, j:j + 1])
                last.then_inc(a_k, 1)

            def step_a(i, p):
                if live(i + 1):
                    queries(i + 1, 1 - p)
                if live(i):
                    exps(i, p, L, SELF_SCALE, a_diff, a_norm, a_exp)
                if live(i + 1):
                    values(i + 1, 1 - p)
                if live(i - 1):
                    even_heads_out(i - 1, 1 - p)
                if live(i + 1):
                    keys(i + 1, 1 - p)
                if live(i + 2):
                    x_t(i + 2, p, a_xt_ps, a_k_ps, a_xt, a_t)
                if isinstance(i, int):
                    if i == 1:
                        eng.wait_ge(in_ident, 16)
                        eng.activation(ident_b[:, :], ident[:, :], ACT.Copy).then_inc(ident_b_made, 1)
                    for n in product_turns.get(i, ()):
                        product_out(n)

            def product_out(n):
                eng.wait_ge(products_ps, n + 1)
                src = bank[n % 3]
                kind, g = product_kinds[n]
                if kind == "ternary":
                    out_t, src = wff_t[:, :, :], src[:, 0:E].bitcast(BF16).rearrange("p (k n) -> p k n", k=KT)
                elif kind == "gamma":
                    out_t, src = gamma_b[:, :], src[:, 0:E]
                elif kind == "keys":
                    out_t, src = wk[:, :, KVC:KVC + R], src[:, 0:KT * R].rearrange("p (k r) -> p k r", k=KT)
                elif kind == "queries":
                    out_t, src = wq_latent[:, 2 * g:2 * g + 2, :].rearrange("q h c -> q (h c)"), src[0:QC, 0:4 * KVC]
                else:
                    out_t, src = wvo[:, 2 * g:2 * g + 2, :].rearrange("q h c -> q (h c)"), src[:, :]
                eng.activation(out_t, src, ACT.Copy).then_inc(products, 1)

            sweep(eng, step_a, 2)

            def keys_out(t, p):
                eng.wait_ge(b_k_ps, t + 1)
                need(eng, b_st_ps, t - 1)
                need(eng, b_k, t)
                eng.activation(kall[:, p, 0, :], b_kp, ACT.Copy)
                for to, half in halves[2:]:
                    last = eng.activation(k_sw[to, :], b_kp[half, :], ACT.Copy)
                last.then_inc(b_k_out, 1)

            def keys_turned(t, p):
                eng.wait_ge(b_k, t + 1)
                for s in range(2):
                    last = eng.activation(kall[rows[s], p, 1, :], kall[rows[1 - s], p, 0, :], ACT.Copy)
                last.then_inc(b_k_turned, 1)

            def keys_rows(t, p):
                eng.wait_ge(b_kvn_ps, t + 1)
                need(eng, b_c_ps, t - 1)
                eng.activation(kvn[:, p, :], b_kvnp, ACT.Copy).then_inc(b_kvn, 1)

            def scores_t(t, p):
                eng.wait_ge(b_st_ps, t + 1)
                need(eng, b_s_ps, t - 1)
                eng.activation(st[:, p, :].rearrange("p (h s q) -> p s h q", h=HP, s=2),
                               quad[:, 0:2, :].rearrange("p s (h q) -> p s h q", h=HP), ACT.Copy).then_inc(b_st, 1)

            def p_t(t, p, s):
                eng.wait_ge(b_pt_ps, 2 * t + s + 1)
                need(eng, b_c_ps, t - 1)
                eng.activation(pt[:, p, 512 * s:512 * s + 512], quad[:, s, :], ACT.Copy).then_inc(b_pt, 1)

            def q_c(t, p):
                eng.wait_ge(b_qc_ps, t + 1)
                need(eng, b_q_ps, 4 * (t - 1))
                eng.activation(qct[:, p, :], b_qcp, ACT.Copy).then_inc(b_qc, 1)

            def contexts(t, p):
                eng.wait_ge(b_c_ps, t + 1)
                need(eng, b_y_ps, t - 1)
                eng.activation(ctxo[:, p, :, :].rearrange("p h (b q) -> p b h q", b=BPT),
                               quad[:, 2:4, :].rearrange("p b (h q) -> p b h q", h=HP), ACT.Copy).then_inc(b_c, 1)

            def queries_rope_out(t, p, g):
                eng.wait_ge(b_q_ps, 4 * t + g + 1)
                need(eng, b_st_ps, t - 1)
                need(eng, (b_q_first, b_q_second)[g], 2 * t)
                eng.activation(q_rope[:, 4 * g:4 * g + 4, :].rearrange("p h t -> p (h t)"), bank[g][:, :], ACT.Copy).then_inc(b_q_out, 1)

            def queries_latent_out(t, p, g):
                eng.wait_ge(b_q_ps, 4 * t + g + 3)
                for s in range(2):
                    last = eng.activation(q_heads[p][rows[s], s, 4 * g:4 * g + 4, :],
                                          bank[g][rows[s], :].rearrange("p (h t) -> p h t", h=4), ACT.Copy)
                last.then_inc(b_q_out, 1)

            def squares(t, p):
                eng.wait_ge(c_h, t + 1)
                need(eng, c_vq, t - 1)
                eng.activation(hsq[:, p, :], h3[:, p, :], ACT.Square, accum_out=ssq[:, p, :]).then_inc(c_ssq, 1)
                eng.wait_ge(c_ssq, t + 1)
                need(eng, c_rq, t - 1)
                eng.activation(vq[:, p, :], ssq[:, p, :], ACT.Copy, scale=1.0 / E, bias=Q_EPS).then_inc(c_vq, 1)

            def x_q_t(t, p):
                eng.wait_ge(c_t_ps, t + 1)
                need(eng, c_y_ps, t - 1)
                eng.activation(xqt[:, p, :, :], c_tp, ACT.Copy).then_inc(c_t, 1)

            def step_b(i, p):
                first = isinstance(i, int) and i == 0
                last = isinstance(i, int) and i >= NT
                if live(i) and not first:
                    scores_t(i, p)
                if live(i + 1):
                    queries_rope_out(i + 1, 1 - p, 0)
                    queries_rope_out(i + 1, 1 - p, 1)
                if live(i - 2) and not last:
                    squares(i - 2, p)
                if first:
                    scores_t(i, p)
                if live(i + 1):
                    keys_turned(i + 1, 1 - p)
                if live(i - 1):
                    p_t(i - 1, 1 - p, 0)
                    p_t(i - 1, 1 - p, 1)
                if last and live(i - 2):
                    squares(i - 2, p)
                if live(i + 2):
                    keys_out(i + 2, p)
                    x_t(i + 2, p, b_xt_ps, b_qc_ps, b_xt, b_t)
                if live(i + 1):
                    queries_latent_out(i + 1, 1 - p, 0)
                if live(i - 1):
                    contexts(i - 1, 1 - p)
                if live(i + 2):
                    q_c(i + 2, p)
                if live(i + 1):
                    keys_rows(i + 1, 1 - p)
                    queries_latent_out(i + 1, 1 - p, 1)
                if live(i):
                    exps(i, p, N, CROSS_SCALE, b_diff, b_norm, b_exp)
                if live(i - 2):
                    x_q_t(i - 2, p)

            sweep(eng, step_b, 3)

        @block.tensor
        def _(eng):
            def transpose_x(t, p, ready, freed, free_at, dst, done):
                eng.wait_ge(ready, t + 1)
                need(eng, freed, free_at)
                for k in range(KT):
                    last = eng.transpose(dst[:, k, :], xh[:, p, k * P:(k + 1) * P], ident[:, :])
                last.then_inc(done, 1)

            def project_xt(t, p, dst, f0, used, done):
                need(eng, used, t)
                for f in range(KT):
                    for k in range(KT):
                        last = eng.matmul(dst[:, f, :], wqkv[:, k, (f0 + f) * P:(f0 + f + 1) * P], xt[:, p, k, :],
                                          start=k == 0, stop=k == KT - 1)
                last.then_inc(done, 1)

            def queries_a(t, p):
                eng.wait_ge(a_xt, t + 1)
                if isinstance(t, int) and t == 0:
                    eng.wait_ge(in_wqkv, 32)
                project_xt(t, p, a_qp, 0, a_q, a_q_ps)

            def values_a(t, p):
                for k in range(KT):
                    last = eng.matmul(a_vp, xt[:, p, k, :], wqkv[:, k, 2 * E:3 * E], start=k == 0, stop=k == KT - 1)
                last.then_inc(a_v_ps, 1)

            def keys_a(t, p):
                project_xt(t, p, a_kp, KT, a_k, a_k_ps)

            def scores_a(t, p):
                eng.wait_ge(a_q, t + 1)
                eng.wait_ge(a_k, t + 1)
                need(eng, a_masked, t)
                need(eng, a_o, t - 1)
                eng.sem_inc(pe_begun, 1)
                for g in range(2):
                    for n in range(NPT):
                        for r in range(4):
                            last = eng.matmul(quad[32 * n:32 * n + 32, r, g * 64:g * 64 + 64],
                                              qt[32 * r:32 * r + 32, p, g, 32 * n:32 * n + 32],
                                              kx[32 * r:32 * r + 32, p, g, :, 32 * n:32 * n + 32],
                                              start=True, stop=True)
                last.then_inc(a_s_ps, 1)

            def weigh_a(t, p):
                eng.wait_ge(a_masked, upto(t + 2))
                eng.wait_ge(a_v, t + 1)
                eng.wait_ge(a_pt, t + 1)
                eng.sem_inc(pe_begun, 1)
                ptv = pt[:, p, 0:512].rearrange("p (r g c) -> p r g c", r=4, g=2)
                for g in range(2):
                    for r in range(4):
                        for n in range(NPT):
                            last = eng.matmul(quad[32 * r:32 * r + 32, n, g * 64:g * 64 + 64],
                                              vs[32 * n:32 * n + 32, p, 32 * (4 * g + r):32 * (4 * g + r) + 32],
                                              ptv[32 * n:32 * n + 32, r, g, :], start=True, stop=True)
                last.then_inc(a_o_ps, 1)

            def project_a(t, p):
                eng.wait_ge(a_o, t + 1)
                need(eng, a_x1, t)
                if isinstance(t, int) and t == 0:
                    eng.wait_ge(in_wout, 16)
                for k in range(KT):
                    last = eng.matmul(a_y, ot[:, p, k, :], wout[:, k, :], start=k == 0, stop=k == KT - 1)
                last.then_inc(a_y_ps, 1)

            def product(n):
                kind, g = product_kinds[n]
                dst = bank[n % 3]
                if n < 3:
                    eng.wait_ge((a_v, a_q, a_k)[n], NT)
                else:
                    eng.wait_ge(products, n - 2)
                if kind == "ternary":
                    eng.wait_ge(ident_b_made, 1)
                    eng.wait_ge(ternary_steps, 6)
                    turned = dst[:, 0:E].bitcast(BF16).rearrange("p (k n) -> p k n", k=KT)
                    for k in range(KT):
                        for m in range(KT):
                            last = eng.transpose(turned[:, k, m * P:(m + 1) * P], wff_q[:, m, k * P:(k + 1) * P], ident_b[:, :])
                elif kind == "gamma":
                    for m in range(KT):
                        last = eng.matmul(dst[:, m * P:(m + 1) * P], ones[:, :], gamma_d[:, m, :], start=True, stop=True)
                elif kind == "keys":
                    eng.wait_ge(in_cross_w, 16 * 12)
                    for k in range(KT):
                        last = eng.matmul(dst[:, k * R:(k + 1) * R], wkvc_t[:, k * P:(k + 1) * P], wkr[:, :], start=True, stop=True)
                elif kind == "queries":
                    for h in range(4):
                        last = eng.matmul(dst[0:QC, h * KVC:(h + 1) * KVC], wuq_t[:, 4 * g + h, :], wuk_t[:, 4 * g + h, :],
                                          start=True, stop=True)
                else:
                    for h in range(4):
                        c = 64 * (h % 2)
                        last = eng.matmul(dst[c:c + KVC, (h // 2) * E:(h // 2 + 1) * E], wuv_t[:, 4 * g + h, :], wo[:, 4 * g + h, :],
                                          start=True, stop=True)
                last.then_inc(products_ps, 1)

            def step_a(i, p):
                if live(i):
                    scores_a(i, p)
                if live(i + 1):
                    queries_a(i + 1, 1 - p)
                    values_a(i + 1, 1 - p)
                last_steps = isinstance(i, int) and i >= NT
                if last_steps and live(i - 2):
                    project_a(i - 2, p)
                if live(i - 1):
                    weigh_a(i - 1, 1 - p)
                if live(i + 1):
                    keys_a(i + 1, 1 - p)
                if live(i - 2) and not last_steps:
                    project_a(i - 2, p)
                if live(i + 2):
                    need(eng, a_v, i + 2)
                    transpose_x(i + 2, p, a_xh, a_xt, i + 2, a_t, a_xt_ps)
                if isinstance(i, int):
                    for n in product_turns.get(i, ()):
                        product(n)

            eng.wait_ge(in_ident, 16)
            sweep(eng, step_a, 2)

            def keys(t, p):
                eng.wait_ge(ctx_in[p], nth(t, p))
                need(eng, b_kvn, t - 1)
                need(eng, c_ffs, t - 4)
                for k in range(KT):
                    last = eng.matmul(b_kp, wk[:, k, :], ctxt[:, p, k, :], start=k == 0, stop=k == KT - 1)
                last.then_inc(b_k_ps, 1)

            def key_rows(t, p):
                eng.wait_ge(b_k_out, upto(t + 2))
                need(eng, c_ffs, t - 3)
                for k in range(KT):
                    last = eng.matmul(b_kvnp, ctxt[:, p, k, :], wk[:, k, 0:KVC], start=k == 0, stop=k == KT - 1)
                last.then_inc(b_kvn_ps, 1)

            def q_c(t, p):
                eng.wait_ge(b_xt, t + 1)
                for k in range(KT):
                    last = eng.matmul(b_qcp, wdq[:, k, :], xt[:, p, k, :], start=k == 0, stop=k == KT - 1)
                last.then_inc(b_qc_ps, 1)

            def queries(t, p, kind, groups):
                w = (wq_rope, wq_latent)[kind]
                eng.wait_ge(b_qc, t + 1)
                for g in groups:
                    need(eng, b_q_out, 4 * t + 2 * kind + g - 1)
                    for h in range(4):
                        last = eng.matmul(bank[g][:, h * P:(h + 1) * P], w[:, 4 * g + h, :], qct[:, p, :],
                                          start=True, stop=True)
                    last.then_inc(b_q_ps, 1)

            def scores_b(t, p):
                eng.wait_ge(b_q_out, 4 * t + 4)
                eng.wait_ge(b_q_first, 2 * t + 2)
                eng.wait_ge(b_q_second, 2 * t + 2)
                eng.wait_ge(b_k_turned, t + 1)
                need(eng, b_pt, 2 * (t - 1))
                eng.sem_inc(pe_begun, 1)
                for s in range(2):
                    for b in range(BPT):
                        last = eng.matmul(quad[64 * b:64 * b + 64, s, :].rearrange("p (h q) -> p h q", h=HP),
                                          kall[:, p, s, 64 * b:64 * b + 64], q_heads[p][:, s, :, 64 * b:64 * b + 64],
                                          start=True, stop=True)
                last.then_inc(b_st_ps, 1)

            def turn_scores(t, p):
                eng.wait_ge(b_st, t + 1)
                need(eng, b_c, t - 1)
                for h in range(HP):
                    last = eng.transpose(quad[:, 2 + h // 4, h % 4 * P:(h % 4 + 1) * P], st[:, p, h * P:(h + 1) * P], ident[:, :])
                last.then_inc(b_s_ps, 1)

            def turn_p(t, p, s):
                eng.wait_ge(b_norm, t + 1)
                eng.wait_ge(b_st, upto(t + 2))
                for h in range(4):
                    last = eng.transpose(quad[:, s, h * P:(h + 1) * P], pn[:, p, (4 * s + h) * P:(4 * s + h + 1) * P],
                                         ident[:, :])
                last.then_inc(b_pt_ps, 1)

            def weigh_b(t, p):
                eng.wait_ge(b_kvn, t + 1)
                eng.wait_ge(b_pt, 2 * t + 2)
                eng.wait_ge(b_masked, upto(t + 2))
                eng.sem_inc(pe_begun, 1)
                pv = pt[:, p, :].rearrange("p (h s q) -> p h s q", h=HP, s=2)
                for s in range(2):
                    for b in range(BPT):
                        rows = slice(64 * b, 64 * b + 64)
                        last = eng.matmul(quad[64 * s:64 * s + 64, 2 + b, :].rearrange("p (h q) -> p h q", h=HP),
                                          kvn[rows, p, :], pv[rows, :, s, :], start=True, stop=True)
                last.then_inc(b_c_ps, 1)

            def project_b(t, p):
                eng.wait_ge(b_c, t + 1)
                eng.wait_ge(b_qc, upto(t + 4))
                for h in range(HP):
                    last = eng.matmul(b_y, ctxo[:, p, h, :], wvo[:, h, :], start=h == 0, stop=h == HP - 1)
                last.then_inc(b_y_ps, 1)

            def turn_quantised(t, p):
                eng.wait_ge(b_k_out, upto(t + 5))
                eng.wait_ge(b_kvn, upto(t + 4))
                need(eng, c_ffs, t)
                eng.wait_ge(c_xq, t + 1)
                for k in range(KT):
                    last = eng.transpose(c_tp[:, k, :], xq[:, p, k * P:(k + 1) * P], ident_b[:, :])
                last.then_inc(c_t_ps, 1)

            def feed_forward(t, p):
                eng.wait_ge(c_t, t + 1)
                for k in range(KT):
                    last = eng.matmul(c_yp, xqt[:, p, k, :], wff_t[:, k, :], start=k == 0, stop=k == KT - 1)
                last.then_inc(c_y_ps, 1)

            def step_b(i, p):
                first = isinstance(i, int) and i == 0
                if live(i) and not first:
                    scores_b(i, p)
                if live(i + 1):
                    queries(i + 1, 1 - p, 0, range(2))
                if first:
                    scores_b(i, p)
                if live(i):
                    turn_scores(i, p)
                if live(i - 1):
                    turn_p(i - 1, 1 - p, 0)
                    turn_p(i - 1, 1 - p, 1)
                if live(i + 2):
                    keys(i + 2, p)
                    transpose_x(i + 2, p, b_xh, c_x2, i - 1, b_t, b_xt_ps)
                if live(i + 1):
                    queries(i + 1, 1 - p, 1, (0,))
                if live(i - 1):
                    weigh_b(i - 1, 1 - p)
                if live(i + 2):
                    q_c(i + 2, p)
                if live(i + 1):
                    key_rows(i + 1, 1 - p)
                    queries(i + 1, 1 - p, 1, (1,))
                late = isinstance(i, int) and i >= NT - 1
                if live(i - 2) and not late:
                    turn_quantised(i - 2, p)
                if live(i - 1):
                    project_b(i - 1, 1 - p)
                if live(i - 2):
                    if late:
                        turn_quantised(i - 2, p)
                    feed_forward(i - 2, p)

            eng.wait_ge(products, 11)
            sweep(eng, step_b, 3)

        @block.vector
        def _(eng):
            def setup_a(i):
                if i == 1:
                    eng.wait_ge(in_window, 32)
                    eng.tensor_copy(seg_f[:, :, :], seg_i[:, :, :]).then_inc(seg_made, 1)
                    eng.wait_ge(in_ffn_w, 32)
                    eng.tensor_reduce(gamma[:, :], wff[:, :, :], AX.X, ALU.add, apply_absolute_value=True).then_inc(ternary_steps, 1)
                    eng.wait_ge(ternary_steps, 1)
                    eng.tensor_scalar(gamma_e[:, :], gamma[:, :], 1.0 / E, Q_EPS, ALU.mult, ALU.add).then_inc(ternary_steps, 1)
                if i == 2:
                    eng.wait_ge(ternary_steps, 2)
                    eng.reciprocal(gamma_r[:, :], gamma_e[:, :]).then_inc(ternary_steps, 1)
                    eng.wait_ge(ternary_steps, 3)
                    for k in range(KT):
                        eng.tensor_scalar(wff_n[:, k, :], wff[:, k, :], gamma_r[:, k:k + 1], ROUND, ALU.mult, ALU.add)
                        last = eng.tensor_scalar(gamma_d[:, k, :], ident[:, :], gamma[:, k:k + 1], 1.0 / E, ALU.mult, ALU.mult)
                    last.then_inc(ternary_steps, 1)
                if i == 3:
                    eng.wait_ge(ternary_steps, 4)
                    eng.tensor_scalar(wff[:, :, :], wff_n[:, :, :], ROUND + 1.0, ROUND - 1.0, ALU.min, ALU.max).then_inc(ternary_steps, 1)
                    eng.wait_ge(ternary_steps, 5)
                    eng.tensor_scalar(wff_q[:, :, :], wff[:, :, :], -ROUND, None, ALU.add).then_inc(ternary_steps, 1)
                if i == NT + 1:
                    eng.wait_ge(window_steps, 1)
                    eng.tensor_scalar(window2, window[:, :, :], 0.0, NEG, ALU.is_gt, ALU.mult).then_inc(window_steps, 1)
                    eng.wait_ge(window_steps, 2)
                    eng.tensor_scalar(window[:, :, :], window[:, :, :], -float(LOOKBACK), NEG, ALU.is_lt, ALU.mult).then_inc(window_steps, 1)
                    eng.wait_ge(window_steps, 3)
                    eng.tensor_tensor(window[:, :, :], window[:, :, :], window2, ALU.add).then_inc(window_steps, 1)

            def statistics(t, p, src, arrived, count, stt, mvt, done, mean, normed):
                if arrived is not None:
                    eng.wait_ge(arrived, count)
                eng.bn_stats(stt[:, p, :], src).then_inc(done, 1)
                eng.wait_ge(done, t + 1)
                eng.sem_inc(dve_begun, 1)
                eng.bn_aggr(mvt[:, p, :], stt[:, p, :]).then_inc(mean, 1)

            def standardise(t, p, src, mvt, rt, dst, ready, used, used_at, done):
                eng.wait_ge(ready, t + 1)
                need(eng, used, used_at)
                eng.tensor_scalar(dst[:, p, :], src, mvt[:, p, 0:1], rt[:, p, :], ALU.subtract, ALU.mult).then_inc(done, 1)

            def mask_a(t, p):
                if isinstance(t, int) and t == 0:
                    eng.wait_ge(in_masks, 32)
                eng.wait_ge(a_s_ps, t + 1)
                need(eng, a_diff, t - 1)
                eng.tensor_tensor(sm[:, p, 0:512].rearrange("p (r g m) -> p r g m", r=4, g=4),
                                  quad[:, :, 0:P].rearrange("p r (g m) -> p r g m", g=4),
                                  causal[:, None, None, :].to_broadcast([P, 4, 4, L]), ALU.add).then_inc(a_masked, 1)

            def row_max(t, p, width, masked, done):
                eng.wait_ge(masked, t + 1)
                eng.tensor_reduce(mx[:, p, :], sm[:, p, 0:H * width].rearrange("p (h k) -> p h k", h=H),
                                  AX.X, ALU.max).then_inc(done, 1)

            def row_sum(t, p, width, exped, summed, done):
                eng.wait_ge(exped, t + 1)
                eng.tensor_reduce(rs[:, p, :], pe[:, p, 0:H * width].rearrange("p (h k) -> p h k", h=H),
                                  AX.X, ALU.add).then_inc(summed, 1)
                eng.wait_ge(summed, t + 1)
                eng.reciprocal(ri[:, p, :], rs[:, p, :]).then_inc(done, 1)

            def turn_p(t, p):
                eng.wait_ge(a_norm, t + 1)
                need(eng, a_o_ps, t - 1)
                eng.transpose(pt[:, p, 0:512], pn[:, p, 0:512]).then_inc(a_pt, 1)

            def residual_a(t, p):
                eng.wait_ge(a_y_ps, t + 1)
                if live(t - 2):
                    eng.wait_ge(x1_out[p], nth(t - 2, p))
                eng.tensor_tensor(x1[:, p, :], a_y, xall[:, t, :], ALU.add).then_inc(a_x1, 1)

            def merge_heads(t, p):
                eng.wait_ge(a_o_even, t + 1)
                need(eng, a_y_ps, t - 1)
                for g in range(KT):
                    last = eng.scalar_tensor_tensor(ot[:, p, g, :].rearrange("p (n l) -> p n l", n=NPT), heads[:, :, g, 1, :],
                                                    parity[:, 1:2], ot_even[:, p, g * P:(g + 1) * P].rearrange("p (n l) -> p n l", n=NPT),
                                                    ALU.mult, ALU.add)
                last.then_inc(a_o, 1)

            def step_a(i, p):
                for t, parity_t in self_finished(i, p):
                    residual_a(t, parity_t)
                if live(i):
                    mask_a(i, p)
                    row_max(i, p, L, a_masked, a_max)
                if live(i + 2):
                    statistics(i + 2, p, xall[:, i + 2, :], x_in[p], nth(i + 2, p), stat, mv, a_stat, a_mean, a_xh)
                if live(i + 2):
                    standardise(i + 2, p, xall[:, i + 2, :], mv, rstd, xh, a_rstd, a_xt_ps, i + 1, a_xh)
                if live(i):
                    row_sum(i, p, L, a_exp, a_sum, a_rec)
                if live(i - 1):
                    merge_heads(i - 1, 1 - p)
                if live(i):
                    turn_p(i, p)
                if isinstance(i, int):
                    setup_a(i)

            eng.wait_ge(fills, 3)
            sweep(eng, step_a, 2)

            def mask_b(t, p):
                if isinstance(t, int) and t == 0:
                    eng.wait_ge(window_steps, 4)
                eng.wait_ge(b_s_ps, t + 1)
                need(eng, b_diff, t - 1)
                eng.tensor_tensor(sm[:, p, :].rearrange("p (h k) -> p h k", h=HP),
                                  quad[:, 2:4, :].rearrange("p s (h k) -> p (s h) k", h=4),
                                  window[:, t, None, :].to_broadcast([P, HP, P]), ALU.add).then_inc(b_masked, 1)

            def rope_keys(t, p):
                eng.wait_ge(b_k_out, t + 1)
                for part, table in ((kall[KVC:, p, 0, :], cos_t), (k_sw[KVC:, :], sin_t)):
                    part = part.rearrange("p (b k) -> p b k", b=BPT)
                    last = eng.tensor_tensor(part, part, table[KVC:, None, :].to_broadcast([R, BPT, N]), ALU.mult)
                last.then_inc(b_k_parts, 1)
                eng.wait_ge(b_k_parts, t + 1)
                eng.tensor_tensor(kall[KVC:, p, 0, :], kall[KVC:, p, 0, :], k_sw[KVC:, :], ALU.add).then_inc(b_k, 1)

            def rope_queries(t, g):
                for part, table in ((q_rope[:, 4 * g:4 * g + 4, :], cos_t), (q_sw[:, 4 * g:4 * g + 4, :], sin_t)):
                    part = part.rearrange("p h (b q) -> p (h b) q", b=BPT)
                    last = eng.tensor_tensor(part, part, table[:, None, :].to_broadcast([P, HP, N]), ALU.mult)
                last.then_inc(b_q_parts, 1)

            def residual_b(t, p):
                eng.wait_ge(b_y_ps, t + 1)
                need(eng, c_x2b, t - 1)
                eng.tensor_tensor(x2[:, p, :], b_y, xall[:, t, :], ALU.add).then_inc(c_x2, 1)

            def largest(t, p):
                eng.wait_ge(c_h, t + 1)
                eng.tensor_reduce(mh[:, p, :], h3[:, p, :], AX.X, ALU.max, apply_absolute_value=True).then_inc(c_mh, 1)

            def quantise(t, p):
                eng.wait_ge(c_rq, t + 1)
                eng.wait_ge(c_mh, t + 1)
                steps = 6 * t
                eng.tensor_scalar(xs[:, p, :], mh[:, p, :], rq[:, p, :], 1.0 / QB, ALU.mult, ALU.mult).then_inc(c_scale, 1)
                eng.wait_ge(c_scale, steps + 1)
                eng.tensor_scalar(xse[:, p, :], xs[:, p, :], Q_EPS, None, ALU.add).then_inc(c_scale, 1)
                eng.wait_ge(c_scale, steps + 2)
                eng.reciprocal(xsr[:, p, :], xse[:, p, :]).then_inc(c_scale, 1)
                eng.wait_ge(c_scale, steps + 3)
                eng.tensor_scalar(hc[:, p, :], h3[:, p, :], rq[:, p, :], None, ALU.mult).then_inc(c_scale, 1)
                eng.wait_ge(c_scale, steps + 4)
                eng.tensor_scalar(hr[:, p, :], hc[:, p, :], xsr[:, p, :], ROUND, ALU.mult, ALU.add).then_inc(c_scale, 1)
                eng.wait_ge(c_scale, steps + 5)
                eng.tensor_scalar(hc[:, p, :], hr[:, p, :], ROUND + QB, ROUND - QB, ALU.min, ALU.max).then_inc(c_scale, 1)
                eng.wait_ge(c_scale, steps + 6)
                need(eng, c_t_ps, t - 1)
                eng.tensor_scalar(xq[:, p, :], hc[:, p, :], -ROUND, None, ALU.add).then_inc(c_xq, 1)

            def finish(t, p):
                eng.wait_ge(c_y_ps, t + 1)
                need(eng, c_out, t - 1)
                if isinstance(t, int) and t == 0:
                    eng.wait_ge(products, 2)
                eng.scalar_tensor_tensor(ffs[:, p, :], c_yp, xs[:, p, :], gamma_b[:, :], ALU.mult, ALU.mult).then_inc(c_ffs, 1)

            def step_b(i, p):
                last = isinstance(i, int) and i == NT + 1
                if live(i - 3) and not last:
                    finish(i - 3, 1 - p)
                if live(i - 2):
                    residual_b(i - 2, p)
                    statistics(i - 2, p, x2[:, p, :], c_x2, i - 1, stat3, mv3, c_stat, c_mean, c_h)
                if last:
                    finish(i - 3, 1 - p)
                if live(i + 2):
                    statistics(i + 2, p, xall[:, i + 2, :], x1_in[p], nth(i + 2, p), stat, mv, b_stat, b_mean, b_xh)
                if live(i - 2):
                    standardise(i - 2, p, x2[:, p, :], mv3, rstd3, h3, c_rstd, c_ssq, i - 3, c_h)
                    largest(i - 2, p)
                if live(i + 2):
                    standardise(i + 2, p, xall[:, i + 2, :], mv, rstd, xh, b_rstd, b_xt_ps, i + 1, b_xh)
                if live(i):
                    mask_b(i, p)
                    row_max(i, p, N, b_masked, b_max)
                    if softmax_on_vector(i):
                        submax(eng, i, p, N, b_max, b_exp, b_diff)
                if live(i - 2):
                    quantise(i - 2, p)
                if live(i + 1):
                    eng.wait_ge(q_swapped, 64 * (i + 2))
                    rope_queries(i + 1, 1)
                    rope_queries(i + 1, 0)
                    eng.wait_ge(b_q_parts, 2 * (i + 1) + 2)
                    add_rope(eng, 1 - p, 0, b_q_first)
                if live(i + 2):
                    rope_keys(i + 2, p)
                if live(i):
                    row_sum(i, p, N, b_exp, b_sum, b_rec)
                    if softmax_on_vector(i):
                        normalise(eng, i, p, N, b_rec, b_pt_ps, 2, b_norm)

            sweep(eng, step_b, 3)


def shape_constants():
    half = R // 2
    inv_freq = (np.float32(1.0) / np.power(np.float32(10000.0), np.arange(half, dtype=np.float32) / np.float32(half))).astype(np.float32)
    ang = (np.arange(N, dtype=np.float32)[:, None] * inv_freq).astype(np.float32)
    cos, sin = np.cos(ang).T, np.sin(ang).T
    row = np.arange(P)
    return {
        "ident_c": np.eye(P, dtype=np.float32),
        "causal_c": np.where(np.arange(L)[None, :] <= (row % L)[:, None], 0.0, NEG).astype(np.float32),
        "parity_c": ((row // DH % 2)[:, None] == np.arange(2)[None, :]).astype(np.float32),
        "cos_c": np.concatenate([cos, cos, cos, cos]).astype(np.float32),
        "sin_c": np.concatenate([-sin, sin, -sin, sin]).astype(np.float32),
        "kidx_c": np.tile(np.arange(N, dtype=np.float32), (P, 1)),
    }


def kernel(x, ctx_2048, itok_BxS_0_1023, L0_attn_weight_qkv, L0_attn_weight_out, L0_xattn_W_kvc, L0_xattn_W_dq,
           L0_xattn_W_uq, L0_xattn_W_qr, L0_xattn_W_uk, L0_xattn_W_kr, L0_xattn_W_uv, L0_xattn_W_o,
           L0_ffn_weight, L0_ffn_bias):
    import concourse.bacc as _bacc
    from concourse.bass_utils import run_bass_kernel_spmd as _run

    lay = np.ascontiguousarray
    a = {
        "x": lay(x),
        "ctx_t": lay(np.asarray(ctx_2048).reshape(NT, P, KT, P).transpose(0, 3, 2, 1).reshape(NT, P, KT * P)),
        "seg": lay(np.tile(np.asarray(itok_BxS_0_1023).reshape(NT, BPT, N).transpose(2, 0, 1), (2, 1, 1))),
        "w_qkv_t": lay(np.asarray(L0_attn_weight_qkv).T),
        "w_out_t": lay(np.asarray(L0_attn_weight_out).T),
        "w_kvc": lay(L0_xattn_W_kvc),
        "w_kvc_t": lay(np.asarray(L0_xattn_W_kvc).T),
        "w_dq": lay(L0_xattn_W_dq),
        "w_uq_t": lay(np.asarray(L0_xattn_W_uq).reshape(QC, H, HD).transpose(2, 1, 0)),
        "w_qr": lay(L0_xattn_W_qr),
        "w_uk_t": lay(np.asarray(L0_xattn_W_uk).reshape(KVC, H, HD).transpose(2, 1, 0)),
        "w_kr": lay(L0_xattn_W_kr),
        "w_uv_t": lay(np.asarray(L0_xattn_W_uv).reshape(KVC, H, HD).transpose(2, 1, 0)),
        "w_o": lay(np.asarray(L0_xattn_W_o).reshape(H, HD, E).transpose(1, 0, 2)),
        "w_ff": lay(L0_ffn_weight),
        "b_ff": lay(np.asarray(L0_ffn_bias).reshape(1, E)),
    }
    a.update(shape_constants())
    nc = _bacc.Bacc("TRN2", target_bir_lowering=False, num_devices=1)
    args = {n: nc.dram_tensor(n, v.shape, mybir.dt.from_np(v.dtype), kind="ExternalInput").ap() for n, v in a.items()}
    x1_dram = nc.dram_tensor("x1_dram", (L, N, E), F32, kind="Internal").ap()
    out = nc.dram_tensor("out", (L, N, E), F32, kind="ExternalOutput").ap()
    decoder_layer(nc, x1_dram=x1_dram, out=out, **args)
    return _run(nc, [a], core_ids=[0]).results[0]["out"]
```
